# Optimizing a Trainium2 kernel written in Bass

```python
import numpy as np
import jax
import jax.numpy as jnp

def _softmax(x, axis=-1):
    return jax.nn.softmax(x, axis=axis)

def _gelu(x):
    return jax.nn.gelu(x, approximate=True)

def _silu(x):
    return jax.nn.silu(x)

def _sigmoid(x):
    return jax.nn.sigmoid(x)

def _layernorm(x, axis=-1, eps=1e-05):
    m = jnp.mean(x, axis=axis, keepdims=True)
    v = jnp.var(x, axis=axis, keepdims=True)
    return (x - m) / jnp.sqrt(v + eps)

def _scatter_add(tgt, idx, src, axis=0):
    return tgt.at[idx].add(src)

def _segment_sum(src, seg, n):
    return jax.ops.segment_sum(src, seg, n)
kernel_name = 'mk_vit_tower_d2_tok_img512_r4_18e1b2'

def setup_inputs(seed: int=0):
    np.random.seed(seed)
    _w = jnp.asarray

    def _rec_inputs():
        import jax
        import jax.numpy as jnp
        _rk = jax.random.key(seed)
        x = -0.000147625 + 0.999875 * jax.random.normal(jax.random.fold_in(_rk, 1), (128, 3, 224, 224), jnp.float32)
        return x
    x = _rec_inputs()

    def _L0_tok_setup():
        import jax, jax.numpy as jnp
        import numpy as np
        N_PATCHES = 8
        PATCH = 28
        C = 3
        IN_D = C * PATCH * PATCH
        HID = 128
        SEQ = N_PATCHES * N_PATCHES + 1

        def _positional_embedding(seq_len, dim):
            i = np.arange(seq_len)[:, None].astype(np.float32)
            j = np.arange(dim)[None, :].astype(np.float32)
            ang = i / np.power(100000.0, j / dim)
            pe = np.where(j % 2 == 0, np.sin(ang), np.cos(ang))
            return jnp.asarray(pe, dtype=jnp.float32)
        key = jax.random.key(seed)
        k1, k2, k3, k4 = jax.random.split(key, 4)
        B = 64
        X = jax.random.normal(k1, (B, C, 224, 224), dtype=jnp.float32)
        bound = 1.0 / np.sqrt(IN_D)
        W = jax.random.uniform(k2, (HID, IN_D), minval=-bound, maxval=bound, dtype=jnp.float32)
        b = jax.random.uniform(k3, (HID,), minval=-bound, maxval=bound, dtype=jnp.float32)
        class_token = jax.random.uniform(k4, (1, HID), dtype=jnp.float32)
        pos_embed = _positional_embedding(SEQ, HID)
        return {'X': X, 'W': W, 'b': b, 'class_token': class_token, 'pos_embed': pos_embed}
    _L0_tok_all = _L0_tok_setup()
    _L0_tok_in = {k: v for k, v in _L0_tok_all.items() if k in ('W', 'b', 'class_token', 'pos_embed')}
    del _L0_tok_all

    def _L0_attn_setup():
        import jax, jax.numpy as jnp
        import numpy as np

        def _positional_encoding(seq_len, hidden):
            pos = jnp.arange(seq_len, dtype=jnp.float32)[:, None]
            div = jnp.exp(jnp.arange(0, hidden, 2, dtype=jnp.float32) * (-jnp.log(10000.0) / hidden))
            ang = pos * div
            return jnp.concatenate([jnp.sin(ang), jnp.cos(ang)], axis=-1)
        key = jax.random.key(seed)
        B, S, H = (8, 512, 128)
        ks = jax.random.split(key, 7)
        s = 1.0 / np.sqrt(H)
        return {'inputs_embeds': jax.random.normal(ks[0], (B, S, H), dtype=jnp.float32), 'Wq': jax.random.uniform(ks[1], (H, H), jnp.float32, -s, s), 'bq': jax.random.uniform(ks[2], (H,), jnp.float32, -s, s), 'Wk': jax.random.uniform(ks[3], (H, H), jnp.float32, -s, s), 'bk': jax.random.uniform(ks[4], (H,), jnp.float32, -s, s), 'Wv': jax.random.uniform(ks[5], (H, H), jnp.float32, -s, s), 'bv': jax.random.uniform(ks[6], (H,), jnp.float32, -s, s)}
    _L0_attn_all = _L0_attn_setup()
    _L0_attn_in = {k: v for k, v in _L0_attn_all.items() if k in ('Wq', 'bq', 'Wk', 'bk', 'Wv', 'bv')}
    del _L0_attn_all

    def _L0_ffn_setup():
        import jax, jax.numpy as jnp
        import numpy as np
        B, S, D = (8, 2048, 128)
        E, DFF = (16, 128)
        CAPACITY = 2
        key = jax.random.key(seed)
        ks = jax.random.split(key, 4)
        x = jax.random.normal(ks[0], (B, S, D), dtype=jnp.float32)
        gate_weight = jax.random.normal(ks[1], (D, E), dtype=jnp.float32) * 0.006
        w1 = jax.random.normal(ks[2], (E, D, DFF), dtype=jnp.float32) * 0.02
        b1 = jnp.zeros((E, DFF), dtype=jnp.float32)
        w2 = jax.random.normal(ks[3], (E, DFF, D), dtype=jnp.float32) * 0.02
        b2 = jnp.zeros((E, D), dtype=jnp.float32)
        return {'x': x, 'gate_weight': gate_weight, 'w1': w1, 'b1': b1, 'w2': w2, 'b2': b2}
    _L0_ffn_all = _L0_ffn_setup()
    _L0_ffn_in = {k: v for k, v in _L0_ffn_all.items() if k in ('gate_weight', 'w1', 'b1', 'w2', 'b2')}
    del _L0_ffn_all

    def _L1_attn_setup():
        import jax, jax.numpy as jnp
        import numpy as np
        import math
        B, S, D, H = (8, 256, 128, 8)
        DH = D // H
        SCALE_BASE = 128

        def _xpos(x, downscale):
            s = x.shape[-2]
            d = x.shape[-1]
            half = d // 2
            sv = (jnp.arange(0, d, 2, dtype=jnp.float32) + 0.4 * d) / (1.4 * d)
            power = jnp.arange(s, dtype=jnp.float32) / SCALE_BASE
            scale = sv[None, :] ** power[:, None]
            inv_freq = 1.0 / 10000.0 ** (jnp.arange(half, dtype=jnp.float32) / half)
            ang = jnp.arange(s, dtype=jnp.float32)[:, None] * inv_freq[None, :]
            if downscale:
                scale = 1.0 / scale
            sin = jnp.repeat(jnp.sin(ang) * scale, 2, axis=-1)
            cos = jnp.repeat(jnp.cos(ang) * scale, 2, axis=-1)
            rot = jnp.stack((-x[..., 1::2], x[..., ::2]), axis=-1).reshape(x.shape)
            return x * cos + rot * sin
        key = jax.random.key(seed)
        ks = jax.random.split(key, 7)
        X = jax.random.normal(ks[0], (B, S, D), dtype=jnp.float32)
        W_Q = jax.random.normal(ks[1], (H, D, DH), dtype=jnp.float32) / D
        W_K = jax.random.normal(ks[2], (H, D, DH), dtype=jnp.float32) / D
        W_V = jax.random.normal(ks[3], (H, D, DH), dtype=jnp.float32) / D
        W_G = jax.random.normal(ks[4], (D, D), dtype=jnp.float32) / D
        W_O = jax.random.normal(ks[5], (D, D), dtype=jnp.float32) / D
        gn_weight = jnp.ones((D,), dtype=jnp.float32)
        gn_bias = jnp.zeros((D,), dtype=jnp.float32)
        return {'X': X, 'W_Q': W_Q, 'W_K': W_K, 'W_V': W_V, 'W_G': W_G, 'W_O': W_O, 'gn_weight': gn_weight, 'gn_bias': gn_bias}
    _L1_attn_all = _L1_attn_setup()
    _L1_attn_in = {k: v for k, v in _L1_attn_all.items() if k in ('W_Q', 'W_K', 'W_V', 'W_G', 'W_O', 'gn_weight', 'gn_bias')}
    del _L1_attn_all

    def _L1_ffn_setup():
        import jax, jax.numpy as jnp
        import numpy as np
        B, S, D, H, E = (4, 512, 128, 256, 8)
        key = jax.random.key(seed)
        ks = jax.random.split(key, 4)
        x = jax.random.normal(ks[0], (B, S, D), jnp.float32)
        Wr = jax.random.normal(ks[1], (E, D), jnp.float32) * 0.02
        br = jnp.zeros((E,), jnp.float32)
        W1 = jax.random.normal(ks[2], (E, D, H), jnp.float32) * 0.02
        b1 = jnp.zeros((E, H), jnp.float32)
        W2 = jax.random.normal(ks[3], (E, H, D), jnp.float32) * 0.02
        b2 = jnp.zeros((E, D), jnp.float32)
        return {'x': x, 'Wr': Wr, 'br': br, 'W1': W1, 'b1': b1, 'W2': W2, 'b2': b2}
    _L1_ffn_all = _L1_ffn_setup()
    _L1_ffn_in = {k: v for k, v in _L1_ffn_all.items() if k in ('Wr', 'br', 'W1', 'b1', 'W2', 'b2')}
    del _L1_ffn_all
    return {'x': x, 'L0_tok_W': _L0_tok_in['W'], 'L0_tok_b': _L0_tok_in['b'], 'L0_tok_class_token': _L0_tok_in['class_token'], 'L0_tok_pos_embed': _L0_tok_in['pos_embed'], 'L0_attn_Wq': _L0_attn_in['Wq'], 'L0_attn_bq': _L0_attn_in['bq'], 'L0_attn_Wk': _L0_attn_in['Wk'], 'L0_attn_bk': _L0_attn_in['bk'], 'L0_attn_Wv': _L0_attn_in['Wv'], 'L0_attn_bv': _L0_attn_in['bv'], 'L0_ffn_gate_weight': _L0_ffn_in['gate_weight'], 'L0_ffn_w1': _L0_ffn_in['w1'], 'L0_ffn_b1': _L0_ffn_in['b1'], 'L0_ffn_w2': _L0_ffn_in['w2'], 'L0_ffn_b2': _L0_ffn_in['b2'], 'L1_attn_W_Q': _L1_attn_in['W_Q'], 'L1_attn_W_K': _L1_attn_in['W_K'], 'L1_attn_W_V': _L1_attn_in['W_V'], 'L1_attn_W_G': _L1_attn_in['W_G'], 'L1_attn_W_O': _L1_attn_in['W_O'], 'L1_attn_gn_weight': _L1_attn_in['gn_weight'], 'L1_attn_gn_bias': _L1_attn_in['gn_bias'], 'L1_ffn_Wr': _L1_ffn_in['Wr'], 'L1_ffn_br': _L1_ffn_in['br'], 'L1_ffn_W1': _L1_ffn_in['W1'], 'L1_ffn_b1': _L1_ffn_in['b1'], 'L1_ffn_W2': _L1_ffn_in['W2'], 'L1_ffn_b2': _L1_ffn_in['b2']}

def reference(x, L0_tok_W, L0_tok_b, L0_tok_class_token, L0_tok_pos_embed, L0_attn_Wq, L0_attn_bq, L0_attn_Wk, L0_attn_bk, L0_attn_Wv, L0_attn_bv, L0_ffn_gate_weight, L0_ffn_w1, L0_ffn_b1, L0_ffn_w2, L0_ffn_b2, L1_attn_W_Q, L1_attn_W_K, L1_attn_W_V, L1_attn_W_G, L1_attn_W_O, L1_attn_gn_weight, L1_attn_gn_bias, L1_ffn_Wr, L1_ffn_br, L1_ffn_W1, L1_ffn_b1, L1_ffn_W2, L1_ffn_b2):
    import jax
    import jax.numpy as jnp

    def _L0_tok_ref(X, W, b, class_token, pos_embed):
        import jax, jax.numpy as jnp
        import numpy as np
        N_PATCHES = 8
        PATCH = 28
        C = 3
        IN_D = C * PATCH * PATCH
        HID = 128
        SEQ = N_PATCHES * N_PATCHES + 1

        def _positional_embedding(seq_len, dim):
            i = np.arange(seq_len)[:, None].astype(np.float32)
            j = np.arange(dim)[None, :].astype(np.float32)
            ang = i / np.power(100000.0, j / dim)
            pe = np.where(j % 2 == 0, np.sin(ang), np.cos(ang))
            return jnp.asarray(pe, dtype=jnp.float32)
        B = X.shape[0]
        patches = X.reshape(B, C, N_PATCHES, PATCH, N_PATCHES, PATCH)
        patches = patches.transpose(0, 2, 4, 1, 3, 5).reshape(B, N_PATCHES * N_PATCHES, IN_D)
        tokens = jnp.einsum('bpi,hi->bph', patches, W) + b
        cls = jnp.broadcast_to(class_token[None, :, :], (B, 1, HID))
        tokens = jnp.concatenate([cls, tokens], axis=1)
        return tokens * pos_embed[None, :, :]

    def _L0_attn_ref(inputs_embeds, Wq, bq, Wk, bk, Wv, bv):
        import jax, jax.numpy as jnp
        import numpy as np

        def _positional_encoding(seq_len, hidden):
            pos = jnp.arange(seq_len, dtype=jnp.float32)[:, None]
            div = jnp.exp(jnp.arange(0, hidden, 2, dtype=jnp.float32) * (-jnp.log(10000.0) / hidden))
            ang = pos * div
            return jnp.concatenate([jnp.sin(ang), jnp.cos(ang)], axis=-1)
        B, S, H = inputs_embeds.shape
        x = inputs_embeds + _positional_encoding(S, H)[None]
        q = jnp.einsum('bsh,dh->bsd', x, Wq) + bq
        k = jnp.einsum('bsh,dh->bsd', x, Wk) + bk
        v = jnp.einsum('bsh,dh->bsd', x, Wv) + bv
        scores = jnp.einsum('bqd,bkd->bqk', q, k)
        weights = jax.nn.softmax(scores, axis=-1)
        return jnp.einsum('bqk,bkd->bqd', weights, v)

    def _L0_ffn_ref(x, gate_weight, w1, b1, w2, b2):
        import jax, jax.numpy as jnp
        import numpy as np
        B, S, D = (8, 2048, 128)
        E, DFF = (16, 128)
        CAPACITY = 2
        Bx, Sx, Dx = x.shape
        num_experts = gate_weight.shape[1]
        k = Sx // num_experts * CAPACITY
        logits = jnp.einsum('bsd,de->bse', x, gate_weight)
        affinity = jax.nn.softmax(logits, axis=-1).transpose(0, 2, 1)
        gating, index = jax.lax.top_k(affinity, k)
        x_in = jnp.take_along_axis(x[:, None, :, :], index[..., None], axis=2)
        h = jax.nn.gelu(jnp.einsum('bekd,edh->bekh', x_in, w1) + b1[None, :, None, :])
        x_e = jnp.einsum('bekh,ehd->bekd', h, w2) + b2[None, :, None, :]
        weighted = gating[..., None] * x_e
        out = jnp.zeros_like(x)
        idx_flat = index.reshape(Bx, num_experts * k)
        vals_flat = weighted.reshape(Bx, num_experts * k, Dx)
        out = out.at[jnp.arange(Bx)[:, None], idx_flat].add(vals_flat)
        return out

    def _L1_attn_ref(X, W_Q, W_K, W_V, W_G, W_O, gn_weight, gn_bias):
        import jax, jax.numpy as jnp
        import numpy as np
        import math
        B, S, D, H = (8, 256, 128, 8)
        DH = D // H
        SCALE_BASE = 128

        def _xpos(x, downscale):
            s = x.shape[-2]
            d = x.shape[-1]
            half = d // 2
            sv = (jnp.arange(0, d, 2, dtype=jnp.float32) + 0.4 * d) / (1.4 * d)
            power = jnp.arange(s, dtype=jnp.float32) / SCALE_BASE
            scale = sv[None, :] ** power[:, None]
            inv_freq = 1.0 / 10000.0 ** (jnp.arange(half, dtype=jnp.float32) / half)
            ang = jnp.arange(s, dtype=jnp.float32)[:, None] * inv_freq[None, :]
            if downscale:
                scale = 1.0 / scale
            sin = jnp.repeat(jnp.sin(ang) * scale, 2, axis=-1)
            cos = jnp.repeat(jnp.cos(ang) * scale, 2, axis=-1)
            rot = jnp.stack((-x[..., 1::2], x[..., ::2]), axis=-1).reshape(x.shape)
            return x * cos + rot * sin
        b, s, _ = X.shape
        gammas = 1.0 - jnp.exp(jnp.linspace(math.log(1.0 / 32), math.log(1.0 / 128), H)).astype(jnp.float32)
        n = jnp.arange(s)
        Dmat = gammas[:, None, None] ** jnp.abs(n[:, None] - n[None, :]).astype(jnp.float32)
        Q = _xpos(jnp.einsum('bsd,hde->bhse', X, W_Q), False)
        K = _xpos(jnp.einsum('bsd,hde->bhse', X, W_K), True)
        V = jnp.einsum('bsd,hde->bhse', X, W_V)
        scores = jnp.einsum('bhse,bhte->bhst', Q, K)
        p = jax.nn.softmax(scores, axis=-1) * Dmat[None]
        Y = jnp.einsum('bhst,bhte->bhse', p, V)
        Y = jnp.moveaxis(Y, 1, 2).reshape(b, s, H * DH)
        Yg = Y.reshape(-1, H, DH)
        mu = Yg.mean(axis=-1, keepdims=True)
        var = Yg.var(axis=-1, keepdims=True)
        Yn = ((Yg - mu) * jax.lax.rsqrt(var + 1e-05)).reshape(-1, H * DH)
        Yn = (Yn * gn_weight + gn_bias).reshape(b, s, H * DH)
        G = X @ W_G
        swish = G * jax.nn.sigmoid(G)
        return swish * Yn @ W_O

    def _L1_ffn_ref(x, Wr, br, W1, b1, W2, b2):
        import jax, jax.numpy as jnp
        import numpy as np
        B, S, D, H, E = (4, 512, 128, 256, 8)
        b, s, d = x.shape
        n = b * s
        e = Wr.shape[0]
        xf = x.reshape(n, d)
        logits = xf @ Wr.T + br
        probs = jax.nn.softmax(logits, axis=-1)
        top2_prob, top2_idx = jax.lax.top_k(probs, 2)
        comb = jnp.zeros((n, e), x.dtype).at[jnp.arange(n)[:, None], top2_idx].add(top2_prob)
        h = jax.nn.gelu(jnp.einsum('nd,edh->enh', xf, W1) + b1[:, None, :], approximate=False)
        o = jnp.einsum('enh,ehd->end', h, W2) + b2[:, None, :]
        y = jnp.einsum('ne,end->nd', comb, o)
        return y.reshape(b, s, d)
    h = _L0_tok_ref(x, L0_tok_W, L0_tok_b, L0_tok_class_token, L0_tok_pos_embed)
    h = h + _L0_attn_ref(_layernorm(h, axis=-1), L0_attn_Wq, L0_attn_bq, L0_attn_Wk, L0_attn_bk, L0_attn_Wv, L0_attn_bv)
    h = h + _L0_ffn_ref(_layernorm(h, axis=-1), L0_ffn_gate_weight, L0_ffn_w1, L0_ffn_b1, L0_ffn_w2, L0_ffn_b2)
    h = h + _L1_attn_ref(_layernorm(h, axis=-1), L1_attn_W_Q, L1_attn_W_K, L1_attn_W_V, L1_attn_W_G, L1_attn_W_O, L1_attn_gn_weight, L1_attn_gn_bias)
    h = h + _L1_ffn_ref(_layernorm(h, axis=-1), L1_ffn_Wr, L1_ffn_br, L1_ffn_W1, L1_ffn_b1, L1_ffn_W2, L1_ffn_b2)
    return h

_drawn_inputs = setup_inputs


def setup_inputs(seed=0):
    import zlib

    import numpy as np

    out = dict(_drawn_inputs(seed))
    spreads = {'L0_ffn_b1': (0.0, 0.8),
     'L0_ffn_b2': (0.0, 0.566),
     'L1_attn_gn_weight': (1.0, 0.6),
     'L1_attn_gn_bias': (0.0, 0.8),
     'L1_ffn_br': (0.0, 0.374),
     'L1_ffn_b1': (0.0, 0.8),
     'L1_ffn_b2': (0.0, 0.286)}
    factors = {'L0_attn_bk': 64.0,
     'L0_ffn_gate_weight': 4.079,
     'L0_ffn_w1': 8.0,
     'L0_ffn_w2': 8.0,
     'L1_attn_W_Q': 8.0,
     'L1_attn_W_K': 8.0,
     'L1_attn_W_V': 8.0,
     'L1_attn_W_G': 8.0,
     'L1_attn_W_O': 8.0,
     'L1_ffn_W1': 4.635,
     'L1_ffn_W2': 4.083}
    for name, (base, spread) in spreads.items():
        noise = np.random.default_rng([zlib.crc32(name.encode()), seed]).standard_normal(out[name].shape)
        drawn = base * np.exp(spread * noise) if base else spread * noise
        out[name] = jnp.asarray(drawn.astype(out[name].dtype))
    for name, factor in factors.items():
        out[name] = (out[name] * factor).astype(out[name].dtype)
    return out
```

```python
import numpy as np
import concourse.bass as bass
from concourse import mybir
from concourse.alu_op_type import AluOpType as ALU
from contextlib import ExitStack

F32 = mybir.dt.float32
BF16 = mybir.dt.bfloat16
U32 = mybir.dt.uint32
I32 = mybir.dt.int32
ACT = mybir.ActivationFunctionType
X = mybir.AxisListType.X
ds = bass.ds

B = 128
PY = 8
NP = PY * PY
S = NP + 1
D = 128
PATCH = 28
IN_D = 3 * PATCH * PATCH
KC = 19
KP = -(-IN_D // KC)
KLAST = IN_D - (KP - 1) * KC
TI = 8
TN = TI * NP
G = 4
W = G * S
NG = B // G
E0, K0 = 16, 8
E1, H1 = 8, 256
NH, DH = 8, 16
EPS = 1e-5


def bc(ap, axis, n):
    shape = list(ap.shape)
    return ap.unsqueeze(axis).broadcast_to(shape[:axis] + [n] + shape[axis:])


def ticks(eng, count, steps):
    deep = max(k for k, _ in steps)
    head = (deep + 3) // 2 * 2
    for t in range(head):
        for k, step in steps:
            if t >= k:
                step(t - k, (t - k) % 2, (t - k) // 2)
    with eng.Fori(head // 2, count // 2) as i:
        for u in range(2):
            for k, step in steps:
                step(i * 2 + (u - k), (u - k) % 2, i + (u - k) // 2)
    for t in range(count, count + deep):
        for k, step in steps:
            if t - k < count:
                step(t - k, (t - k) % 2, (t - k) // 2)


def wait(eng, sem, n):
    if isinstance(n, int) and n <= 0:
        return
    eng.wait_ge(sem, n)


class Mem:

    def __init__(self, nc, ctx):
        self.nc, self.ctx = nc, ctx

    def sb(self, name, shape, dt=F32):
        return self.ctx.enter_context(self.nc.sbuf_tensor(name, shape, dt))

    def ps(self, name, shape, dt=F32):
        return self.ctx.enter_context(self.nc.psum_tensor(name, shape, dt))

    def sem(self, name):
        return self.ctx.enter_context(self.nc.semaphore(name))


def row_broadcast(dram_row, parts):
    return dram_row.unsqueeze(0).broadcast_to([parts, dram_row.shape[0]])


def patch_tokens(nc, io, st):
    h, stats, ident = st["h"], st["stats"], st["ident"]
    with ExitStack() as ctx:
        m = Mem(nc, ctx)
        w = m.sb("tok_w", [128, KC, D])
        x = [m.sb(f"tok_x{i}", [128, KC, TN]) for i in range(2)]
        tok_t = [m.sb(f"tok_t{i}", [D, TI, S]) for i in range(2)]
        pos_t, bias, cls = m.sb("pos_t", [D, S]), m.sb("tok_bias", [D, 1]), m.sb("tok_cls", [D, 1])
        p_emb = [m.ps(f"p_emb{i}", [D, TI, NP]) for i in range(2)]
        p_tok = [m.ps(f"p_tok{i}", [128, G, D]) for i in range(4)]
        consts_in, x_in = m.sem("tok_consts_in"), [m.sem(f"x_in{i}") for i in range(2)]
        ident0, ident_made = m.sem("ident_zeroed"), m.sem("ident_made")
        embedded, tok_made, cls_made = m.sem("embedded"), m.sem("tok_made"), m.sem("cls_made")
        turned, h_made, stats_made = m.sem("tok_turned"), m.sem("h_made"), m.sem("tok_stats_made")
        NT = B // TI
        with nc.Block() as block:

            @block.sync
            def _(sp):
                sp.dma_start(w[0:KP - 1], io["tok_wt"][0:(KP - 1) * KC, :].rearrange("(p c) n -> p c n", c=KC)).then_inc(consts_in, 16)
                sp.dma_start(w[KP - 1:KP, 0:KLAST], io["tok_wt"][(KP - 1) * KC:IN_D, :].unsqueeze(0)).then_inc(consts_in, 16)
                sp.dma_start(pos_t[:], io["pos_t"]).then_inc(consts_in, 16)
                sp.dma_start(bias[:], io["tok_b"].unsqueeze(1)).then_inc(consts_in, 16)
                sp.dma_start(cls[:], io["cls_t"]).then_inc(consts_in, 16)

                def load(g, p, j2):
                    wait(sp, embedded, g - 1)
                    blk = io["patches"][g] if isinstance(g, int) else io["patches"][ds(g, 1)].squeeze(0)
                    sp.dma_start(x[p][0:KP - 1], blk[0:(KP - 1) * KC, :].rearrange("(p c) n -> p c n", c=KC)).then_inc(x_in[p], 16)
                    sp.dma_start(x[p][KP - 1:KP, 0:KLAST], blk[(KP - 1) * KC:IN_D, :].unsqueeze(0)).then_inc(x_in[p], 16)

                ticks(sp, NT, [(0, load)])

            @block.gpsimd
            def _(pool):
                nc.gpsimd.memset(st["minus_half"][:], -0.5)
                nc.gpsimd.memset(ident[:], 0.0).then_inc(ident0, 1)
                pool.wait_ge(ident0, 1)
                nc.gpsimd.affine_select(out=ident[:], in_=ident[:], compare_op=ALU.not_equal, fill=1.0, base=0,
                                        pattern=[[-1, 128]], channel_multiplier=1).then_inc(ident_made, 1)

            @block.tensor
            def _(pe):
                pe.wait_ge(consts_in, 80)
                pe.wait_ge(ident_made, 1)

                def embed(g, p, j2):
                    pe.wait_ge(x_in[p], j2 * 32 + 32)
                    wait(pe, tok_made, g - 1)
                    for c in range(KC):
                        k = KP if c < KLAST else KP - 1
                        last = nc.tensor.matmul(p_emb[p][:], w[0:k, c, :], x[p][0:k, c, :], start=c == 0, stop=c == KC - 1)
                    last.then_inc(embedded, 1)

                def turn(g, p, j2):
                    pe.wait_ge(tok_made, g + 1)
                    wait(pe, h_made, g - 1)
                    for j in range(TI):
                        last = nc.tensor.transpose(p_tok[2 * p + j // G][0:S, j % G, :], tok_t[p][:, j, :], ident[:])
                    last.then_inc(turned, 1)

                ticks(pe, NT, [(0, embed), (1, turn)])

            @block.vector
            def _(dve):
                dve.wait_ge(consts_in, 80)
                for p in range(2):
                    nc.vector.tensor_tensor(tok_t[p][:, :, 0], bc(cls[:, 0], 1, TI), bc(pos_t[:, 0], 1, TI), ALU.mult).then_inc(cls_made, 1)

                def finish(g, p, j2):
                    dve.wait_ge(embedded, g + 1)
                    wait(dve, turned, g - 1)
                    nc.vector.scalar_tensor_tensor(out=tok_t[p][:, :, 1:S], in0=p_emb[p][:], scalar=bias[:, 0:1], in1=bc(pos_t[:, 1:S], 1, TI),
                                                   op0=ALU.add, op1=ALU.mult).then_inc(tok_made, 1)

                def statistics(g, p, j2):
                    dve.wait_ge(h_made, g + 1)
                    for j in range(TI):
                        last = nc.vector.bn_stats(stats[:, ds(g * TI + j, 1), :].rearrange("p a b -> p (a b)"),
                                                  h[:, ds(g * TI + j, 1), :].rearrange("p a b -> p (a b)"))
                    last.then_inc(stats_made, 1)

                ticks(dve, NT, [(0, finish), (2, statistics)])

            @block.scalar
            def _(act):
                def keep(g, p, j2):
                    act.wait_ge(turned, g + 1)
                    for i in range(2):
                        last = nc.scalar.copy(h[:, ds(g * TI + i * G, G), :], p_tok[2 * p + i][0:S])
                    last.then_inc(h_made, 1)

                ticks(act, NT, [(0, keep)])


def inverse_root(nc, dve, out, v, t, step, base):
    n = base

    def then(ins):
        nonlocal n
        ins.then_inc(step, 1)
        n = n + 1
        dve.wait_ge(step, n)

    then(nc.vector.tensor_scalar(t.bitcast(I32), v.bitcast(I32), 1, None, ALU.logical_shift_right))
    then(nc.vector.tensor_scalar(out.bitcast(I32), t.bitcast(I32), -1.0, float(0x5F3759DF), ALU.mult, ALU.add))
    for _ in range(3):
        then(nc.vector.tensor_tensor(t, out, out, ALU.mult))
        then(nc.vector.scalar_tensor_tensor(out=t, in0=t, scalar=-0.5, in1=v, op0=ALU.mult, op1=ALU.mult))
        then(nc.vector.scalar_tensor_tensor(out=out, in0=t, scalar=1.5, in1=out, op0=ALU.add, op1=ALU.mult))


def ln_statistics(nc, st, m, stage):
    return {"part": m.sb(f"{stage}_ln_part", [S, 4, B]), "sum": m.sem(f"{stage}_ln_sums"), "mid": m.sem(f"{stage}_ln_mid"),
            "var": m.sem(f"{stage}_ln_var"), "step": m.sem(f"{stage}_ln_step"), "st": st}


def ln_on_dve(nc, dve, ln):
    st = ln["st"]
    s6, part = st["stats"], ln["part"]
    nc.vector.tensor_tensor(part[:, 0, :], s6[:, :, 1], s6[:, :, 4], ALU.add)
    nc.vector.tensor_tensor(part[:, 1, :], s6[:, :, 1], s6[:, :, 4], ALU.subtract)
    nc.vector.tensor_tensor(part[:, 2, :], s6[:, :, 2], s6[:, :, 5], ALU.add).then_inc(ln["sum"], 1)
    dve.wait_ge(ln["sum"], 1)
    nc.vector.tensor_scalar(st["mean"][:], part[:, 0, :], 0.5, None, ALU.mult)
    nc.vector.tensor_tensor(part[:, 3, :], part[:, 1, :], part[:, 1, :], ALU.mult)
    nc.vector.tensor_scalar(part[:, 2, :], part[:, 2, :], 1.0 / D, EPS, ALU.mult, ALU.add).then_inc(ln["mid"], 1)
    dve.wait_ge(ln["mid"], 1)
    nc.vector.scalar_tensor_tensor(out=part[:, 1, :], in0=part[:, 3, :], scalar=0.25, in1=part[:, 2, :],
                                   op0=ALU.mult, op1=ALU.add).then_inc(ln["var"], 1)
    dve.wait_ge(ln["var"], 1)
    inverse_root(nc, dve, st["rstd"][:], part[:, 1, :], part[:, 2, :], ln["step"], 0)


def normalise(nc, out, st, b0, count):
    for j in range(count):
        last = nc.vector.tensor_scalar(out[:, j, :], st["h"][:, ds(b0 + j, 1), :].rearrange("p a b -> p (a b)"),
                                       st["mean"][:, ds(b0 + j, 1)], st["rstd"][:, ds(b0 + j, 1)], ALU.subtract, ALU.mult)
    return last


def token_statistics(nc, st, b0, count):
    for j in range(count):
        last = nc.vector.bn_stats(st["stats"][:, ds(b0 + j, 1), :].rearrange("p a b -> p (a b)"),
                                  st["h"][:, ds(b0 + j, 1), :].rearrange("p a b -> p (a b)"))
    return last


def attention(nc, io, st):
    h, ident = st["h"], st["ident"]
    with ExitStack() as ctx:
        m = Mem(nc, ctx)
        wq, wk, wv = m.sb("wq", [D, D]), m.sb("wk", [D, D]), m.sb("wv", [D, D])
        bq, bk, bv = m.sb("bq", [D, 1]), m.sb("bk", [D, 1]), m.sb("bv", [S, D])
        sinus = m.sb("sinus", [D, S])
        xn = [m.sb(f"a_xn{i}", [S, G, D]) for i in range(2)]
        xt = [m.sb(f"a_xt{i}", [D, W]) for i in range(2)]
        qt = [m.sb(f"a_qt{i}", [D, W]) for i in range(2)]
        kt = [m.sb(f"a_kt{i}", [D, W]) for i in range(2)]
        v = [m.sb(f"a_v{i}", [S, G, D]) for i in range(2)]
        neg = [m.sb(f"a_neg{i}", [S, G]) for i in range(2)]
        tot = [m.sb(f"a_tot{i}", [S, G]) for i in range(2)]
        inv = [m.sb(f"a_inv{i}", [S, G]) for i in range(2)]
        ex = [m.sb(f"a_ex{i}", [S, G, S]) for i in range(2)]
        pr = [m.sb(f"a_pr{i}", [S, G, S]) for i in range(2)]
        pt = [m.sb(f"a_pt{i}", [S, G, S]) for i in range(2)]
        p_x, p_q, p_k = m.ps("a_px", [D, W]), m.ps("a_pq", [D, W]), m.ps("a_pk", [D, W])
        p_v, p_s = m.ps("a_pv", [S, G, D]), m.ps("a_ps", [S, G, S])
        p_t, p_o = m.ps("a_ppt", [S, G, S]), m.ps("a_po", [S, G, D])
        ln = ln_statistics(nc, st, m, "a")
        w_in = m.sem("a_weights_in")
        normed, x_turned, x_ready = m.sem("a_normed"), m.sem("a_x_turned"), m.sem("a_x_ready")
        projected, qk_ready, v_ready = m.sem("a_projected"), m.sem("a_qk_ready"), m.sem("a_v_ready")
        scored, maxed, exped, inverted = m.sem("a_scored"), m.sem("a_maxed"), m.sem("a_exped"), m.sem("a_inverted")
        probs_ready, probs_turned, pt_ready = m.sem("a_probs_ready"), m.sem("a_probs_turned"), m.sem("a_pt_ready")
        mixed, added, stats_made = m.sem("a_mixed"), m.sem("a_added"), m.sem("a_stats_made")
        with nc.Block() as block:

            @block.sync
            def _(sp):
                for t, src in ((wq, io["wq_t"]), (wk, io["wk_t"]), (wv, io["wv_t"]), (bq, io["bq"].unsqueeze(1)), (bk, io["bk"].unsqueeze(1)),
                               (bv, row_broadcast(io["bv"], S)), (sinus, io["sinus_t"])):
                    sp.dma_start(t[:], src).then_inc(w_in, 16)

            @block.vector
            def _(dve):
                ln_on_dve(nc, dve, ln)
                dve.wait_ge(w_in, 7 * 16)

                def norm(g, p, j2):
                    wait(dve, x_turned, g - 1)
                    normalise(nc, xn[p], st, g * G, G).then_inc(normed, 1)

                def place(g, p, j2):
                    dve.wait_ge(x_turned, g + 1)
                    wait(dve, projected, g - 1)
                    nc.vector.tensor_tensor(xt[p][:].rearrange("p (a b) -> p a b", a=G), p_x[:].rearrange("p (a b) -> p a b", a=G),
                                            bc(sinus[:], 1, G), ALU.add).then_inc(x_ready, 1)

                def v_bias(g, p, j2):
                    dve.wait_ge(projected, g + 1)
                    wait(dve, mixed, g - 1)
                    nc.vector.tensor_tensor(v[p][:], p_v[:], bc(bv[:], 1, G), ALU.add).then_inc(v_ready, 1)

                def row_max(g, p, j2):
                    dve.wait_ge(scored, g + 1)
                    wait(dve, exped, g - 1)
                    nc.vector.tensor_reduce(neg[p][:], p_s[:], X, ALU.max, negate=True).then_inc(maxed, 1)

                def invert(g, p, j2):
                    dve.wait_ge(exped, g + 1)
                    wait(dve, probs_ready, g - 1)
                    nc.vector.reciprocal(inv[p][:], tot[p][:]).then_inc(inverted, 1)

                def add(g, p, j2):
                    dve.wait_ge(mixed, g + 1)
                    nc.vector.tensor_tensor(h[:, ds(g * G, G), :], h[:, ds(g * G, G), :], p_o[:], ALU.add).then_inc(added, 1)

                def statistics(g, p, j2):
                    dve.wait_ge(added, g + 1)
                    token_statistics(nc, st, g * G, G).then_inc(stats_made, 1)

                ticks(dve, NG, [(3, row_max), (4, add), (0, norm), (3, invert), (4, statistics), (2, v_bias), (1, place)])

            @block.gpsimd
            def _(pool):
                def divide(g, p, j2):
                    pool.wait_ge(inverted, g + 1)
                    wait(pool, probs_turned, g - 1)
                    nc.gpsimd.tensor_tensor(pr[p][:], ex[p][:], bc(inv[p][:], 2, S), ALU.mult).then_inc(probs_ready, 1)

                ticks(pool, NG, [(0, divide)])

            @block.scalar
            def _(act):
                act.wait_ge(w_in, 7 * 16)

                def qk_bias(g, p, j2):
                    act.wait_ge(projected, g + 1)
                    wait(act, scored, g - 1)
                    nc.scalar.activation(qt[p][:], p_q[:], ACT.Identity, bias=bq[:, 0:1])
                    nc.scalar.activation(kt[p][:], p_k[:], ACT.Identity, bias=bk[:, 0:1]).then_inc(qk_ready, 1)

                def exponent(g, p, j2):
                    act.wait_ge(maxed, g + 1)
                    wait(act, probs_ready, g - 1)
                    for j in range(G):
                        last = nc.scalar.activation(ex[p][:, j, :], p_s[:, j, :], ACT.Exp, bias=neg[p][:, j:j + 1], accum_out=tot[p][:, j:j + 1])
                    last.then_inc(exped, 1)

                def keep_pt(g, p, j2):
                    act.wait_ge(probs_turned, g + 1)
                    wait(act, mixed, g - 1)
                    nc.scalar.copy(pt[p][:], p_t[:]).then_inc(pt_ready, 1)

                ticks(act, NG, [(1, exponent), (0, qk_bias), (1, keep_pt)])

            @block.tensor
            def _(pe):
                pe.wait_ge(w_in, 7 * 16)

                def turn_x(g, p, j2):
                    pe.wait_ge(normed, g + 1)
                    wait(pe, x_ready, g)
                    for j in range(G):
                        last = nc.tensor.transpose(p_x[:, j * S:(j + 1) * S], xn[p][:, j, :], ident[0:S, 0:S])
                    last.then_inc(x_turned, 1)

                def project(g, p, j2):
                    pe.wait_ge(x_ready, g + 1)
                    wait(pe, qk_ready, g)
                    wait(pe, v_ready, g)
                    nc.tensor.matmul(p_q[:], wq[:], xt[p][:], start=True, stop=True)
                    nc.tensor.matmul(p_k[:], wk[:], xt[p][:], start=True, stop=True)
                    for j in range(G):
                        last = nc.tensor.matmul(p_v[:, j, :], xt[p][:, j * S:(j + 1) * S], wv[:], start=True, stop=True)
                    last.then_inc(projected, 1)

                def score(g, p, j2):
                    pe.wait_ge(qk_ready, g + 1)
                    wait(pe, exped, g)
                    for j in range(G):
                        c = slice(j * S, (j + 1) * S)
                        last = nc.tensor.matmul(p_s[:, j, :], qt[p][:, c], kt[p][:, c], start=True, stop=True)
                    last.then_inc(scored, 1)

                def turn_probs(g, p, j2):
                    pe.wait_ge(probs_ready, g + 1)
                    wait(pe, pt_ready, g)
                    for j in range(G):
                        last = nc.tensor.transpose(p_t[:, j, :], pr[p][:, j, :], ident[0:S, 0:S])
                    last.then_inc(probs_turned, 1)

                def mix(g, p, j2):
                    pe.wait_ge(pt_ready, g + 1)
                    pe.wait_ge(v_ready, g + 1)
                    wait(pe, added, g)
                    for j in range(G):
                        last = nc.tensor.matmul(p_o[:, j, :], pt[p][:, j, :], v[p][:, j, :], start=True, stop=True)
                    last.then_inc(mixed, 1)

                ticks(pe, NG, [(1, project), (2, turn_probs), (0, turn_x), (1, score), (2, mix)])

def route_to_experts(nc, io, st):
    ident, xg, selt = st["ident"], st["xg"], st["selt"]
    with ExitStack() as ctx:
        m = Mem(nc, ctx)
        gate, iota = m.sb("r_gate", [D, E0]), m.sb("r_iota", [128, S])
        identb = m.sb("r_identb", [128, 128], BF16)
        xn = [m.sb(f"r_xn{i}", [S, TI, D]) for i in range(2)]
        xt = m.sb("r_xt", [D, TI * S])
        neg, tot, inv = m.sb("r_neg", [S, TI]), m.sb("r_tot", [S, TI]), m.sb("r_inv", [S, TI])
        lg, ex, aff = m.sb("r_lg", [S, TI, E0]), m.sb("r_ex", [S, TI, E0]), [m.sb(f"r_aff{i}", [S, TI, E0]) for i in range(2)]
        aft, top = m.sb("r_aft", [128, S]), m.sb("r_top", [128, K0])
        idx, idxf = m.sb("r_idx", [128, K0], U32), m.sb("r_idxf", [128, K0])
        spare = m.sb("r_spare", [128, 1])
        oh = m.sb("r_onehot", [128, K0, S], BF16)
        sel, selw = m.sb("r_sel", [S, TI, K0 * E0]), m.sb("r_selw", [S, TI, K0 * E0])
        p_x = [m.ps(f"r_px{i}", [D, W]) for i in range(2)]
        p_small = m.ps("r_psmall", [128, 512])
        p_l, p_a = p_small[0:S, 0:TI * E0].rearrange("p (a b) -> p a b", a=TI), p_small[:, 256:256 + S]
        p_sel = m.ps("r_psel", [S, K0, 128], BF16)
        p_g = [m.ps(f"r_pg{i}", [D, G, K0, E0]) for i in range(2)]
        p_w = [m.ps(f"r_pw{i}", [128, G, S]) for i in range(2)]
        ln = ln_statistics(nc, st, m, "r")
        w_in, cast = m.sem("r_weights_in"), m.sem("r_identb_made")
        normed, x_turned, x_ready = m.sem("r_normed"), m.sem("r_x_turned"), m.sem("r_x_ready")
        gated, maxed, shifted, exped = m.sem("r_gated"), m.sem("r_maxed"), m.sem("r_shifted"), m.sem("r_exped")
        summed, inverted, aff_ready = m.sem("r_summed"), m.sem("r_inverted"), m.sem("r_aff_ready")
        aff_turned, aft_ready, topped = m.sem("r_aff_turned"), m.sem("r_aft_ready"), m.sem("r_topped")
        indexed, idxf_ready, oh_ready = m.sem("r_indexed"), m.sem("r_idxf_ready"), m.sem("r_onehot_ready")
        oh_turned, sel_ready, selw_ready = m.sem("r_onehot_turned"), m.sem("r_sel_ready"), m.sem("r_selw_ready")
        gathered, xg_kept, selw_turned, selt_kept = m.sem("r_gathered"), m.sem("r_xg_kept"), m.sem("r_selw_turned"), m.sem("r_selt_kept")
        NT = B // TI
        with nc.Block() as block:

            @block.sync
            def _(sp):
                sp.dma_start(gate[:], io["gate"]).then_inc(w_in, 16)
                sp.dma_start(iota[:], row_broadcast(io["iota"], 128)).then_inc(w_in, 16)

            @block.vector
            def _(dve):
                nc.vector.tensor_copy(identb[:], ident[:]).then_inc(cast, 1)
                ln_on_dve(nc, dve, ln)
                dve.wait_ge(w_in, 32)

                def norm(g, p, j2):
                    wait(dve, gathered, g - 1)
                    normalise(nc, xn[p], st, g * TI, TI).then_inc(normed, 1)

                def softmax(g, p, j2):
                    dve.wait_ge(gated, g + 1)
                    nc.vector.tensor_reduce(neg[:], p_l, X, ALU.max, negate=True).then_inc(maxed, 1)
                    dve.wait_ge(maxed, g + 1)
                    wait(dve, exped, g)
                    nc.vector.tensor_tensor(lg[:], p_l, bc(neg[:], 2, E0), ALU.add).then_inc(shifted, 1)

                def divide(g, p, j2):
                    dve.wait_ge(exped, g + 1)
                    nc.vector.tensor_reduce(tot[:], ex[:], X, ALU.add).then_inc(summed, 1)
                    dve.wait_ge(summed, g + 1)
                    nc.vector.reciprocal(inv[:], tot[:]).then_inc(inverted, 1)
                    dve.wait_ge(inverted, g + 1)
                    wait(dve, aff_turned, g - 1)
                    nc.vector.tensor_tensor(aff[p][:], ex[:], bc(inv[:], 2, E0), ALU.mult).then_inc(aff_ready, 1)

                def choose(g, p, j2):
                    dve.wait_ge(aff_turned, g + 1)
                    nc.vector.tensor_copy(aft[:], p_a).then_inc(aft_ready, 1)
                    dve.wait_ge(aft_ready, g + 1)
                    nc.vector.memset(spare[:], 0.0)
                    nc.vector.max(top[:], aft[:]).then_inc(topped, 1)
                    dve.wait_ge(topped, g + 1)
                    nc.vector.memset(spare[:], 0.0)
                    nc.vector.max_index(idx[:], top[:], aft[:]).then_inc(indexed, 1)
                    dve.wait_ge(indexed, g + 1)
                    nc.vector.tensor_copy(idxf[:], idx[:]).then_inc(idxf_ready, 1)
                    dve.wait_ge(idxf_ready, g + 1)
                    wait(dve, oh_turned, g)
                    nc.vector.tensor_tensor(oh[:], bc(iota[:], 1, K0), bc(idxf[:], 2, S), ALU.is_equal).then_inc(oh_ready, 1)

                def weigh(g, p, j2):
                    dve.wait_ge(sel_ready, g + 1)
                    wait(dve, selw_turned, g)
                    nc.vector.tensor_tensor(selw[:].rearrange("p a (k e) -> p a k e", k=K0), sel[:].rearrange("p a (k e) -> p a k e", k=K0),
                                            bc(aff[p][:], 2, K0), ALU.mult).then_inc(selw_ready, 1)

                def keep_selt(g, p, j2):
                    dve.wait_ge(selw_turned, g + 1)
                    for i in range(2):
                        last = nc.vector.tensor_copy(selt[:, ds(g * TI + i * G, G), :], p_w[i][:])
                    last.then_inc(selt_kept, 1)

                ticks(dve, NT, [(2, choose), (1, softmax), (3, keep_selt), (0, norm), (2, weigh), (1, divide)])

            @block.scalar
            def _(act):
                def keep_x(g, p, j2):
                    act.wait_ge(x_turned, g + 1)
                    wait(act, gated, g)
                    for i in range(2):
                        last = nc.scalar.copy(xt[:, i * W:(i + 1) * W], p_x[i][:])
                    last.then_inc(x_ready, 1)

                def exponent(g, p, j2):
                    act.wait_ge(shifted, g + 1)
                    wait(act, aff_ready, g)
                    nc.scalar.activation(ex[:], lg[:], ACT.Exp).then_inc(exped, 1)

                def keep_sel(g, p, j2):
                    act.wait_ge(oh_turned, g + 1)
                    wait(act, selw_ready, g)
                    wait(act, gathered, g)
                    nc.scalar.copy(sel[:].rearrange("p a (k e) -> p k a e", k=K0), p_sel[:].rearrange("p k (a e) -> p k a e", a=TI)).then_inc(sel_ready, 1)

                def keep_g(g, p, j2):
                    act.wait_ge(gathered, g + 1)
                    for i in range(2):
                        last = nc.scalar.copy(xg[:, :, ds(g * TI + i * G, G), :], p_g[i][:].rearrange("p a k e -> p e a k"))
                    last.then_inc(xg_kept, 1)

                ticks(act, NT, [(0, keep_x), (1, keep_sel), (0, exponent), (1, keep_g)])

            @block.tensor
            def _(pe):
                pe.wait_ge(w_in, 32)
                pe.wait_ge(cast, 1)

                def turn_x(g, p, j2):
                    pe.wait_ge(normed, g + 1)
                    wait(pe, x_ready, g)
                    for j in range(TI):
                        last = nc.tensor.transpose(p_x[j // G][:, j % G * S:(j % G + 1) * S], xn[p][:, j, :], ident[0:S, 0:S])
                    last.then_inc(x_turned, 1)

                def gates(g, p, j2):
                    pe.wait_ge(x_ready, g + 1)
                    wait(pe, shifted, g)
                    wait(pe, aft_ready, g)
                    for j in range(TI):
                        last = nc.tensor.matmul(p_l[:, j, :], xt[:, j * S:(j + 1) * S], gate[:], start=True, stop=True)
                    last.then_inc(gated, 1)

                def turn_aff(g, p, j2):
                    pe.wait_ge(aff_ready, g + 1)
                    nc.tensor.transpose(p_a, aff[p][:].rearrange("p a b -> p (a b)"), ident[0:S, 0:S]).then_inc(aff_turned, 1)

                def turn_onehot(g, p, j2):
                    pe.wait_ge(oh_ready, g + 1)
                    wait(pe, sel_ready, g)
                    for k in range(K0):
                        last = nc.tensor.transpose(p_sel[:, k, :], oh[:, k, :], identb[:])
                    last.then_inc(oh_turned, 1)

                def gather(g, p, j2):
                    pe.wait_ge(sel_ready, g + 1)
                    wait(pe, xg_kept, g)
                    for j in range(TI):
                        last = nc.tensor.matmul(p_g[j // G][:, j % G].rearrange("p k e -> p (k e)"), xn[p][:, j, :], sel[:, j, :], start=True, stop=True)
                    last.then_inc(gathered, 1)

                def turn_selw(g, p, j2):
                    pe.wait_ge(selw_ready, g + 1)
                    wait(pe, selt_kept, g)
                    for j in range(TI):
                        last = nc.tensor.transpose(p_w[j // G][:, j % G, :], selw[:, j, :], ident[0:S, 0:S])
                    last.then_inc(selw_turned, 1)

                ticks(pe, NT, [(1, turn_aff), (0, turn_x), (1, turn_onehot), (0, gates), (1, gather), (1, turn_selw)])


def expert_layers(nc, io, st):
    xg = st["xg"]
    N = B * K0 // 2
    with ExitStack() as ctx:
        m = Mem(nc, ctx)
        w1 = [m.sb(f"e_w1_{i}", [D, D]) for i in range(2)]
        w2 = [m.sb(f"e_w2_{i}", [D, D]) for i in range(2)]
        b1, b2 = m.sb("e_b1", [D, E0]), m.sb("e_b2", [D, E0])
        ht = [m.sb(f"e_h{i}", [D, 2, N]) for i in range(2)]
        p_h = [[m.ps(f"e_ph{i}{j}", [D, N]) for j in range(2)] for i in range(2)]
        p_y = [[m.ps(f"e_py{i}{j}", [D, N]) for j in range(2)] for i in range(2)]
        b_in, w_in = m.sem("e_bias_in"), [m.sem(f"e_weights_in{i}") for i in range(2)]
        up_done, h_ready, down_done, y_kept = m.sem("e_up"), m.sem("e_h_ready"), m.sem("e_down"), m.sem("e_y_kept")
        flat = xg[:].rearrange("p e b k -> p e (b k)")
        with nc.Block() as block:

            @block.sync
            def _(sp):
                sp.dma_start(b1[:], io["b1_t"]).then_inc(b_in, 16)
                sp.dma_start(b2[:], io["b2_t"]).then_inc(b_in, 16)

                def load(g, p, j2):
                    wait(sp, down_done, g - 1)
                    for t, src in ((w1, io["w1"]), (w2, io["w2"])):
                        sp.dma_start(t[p][:], src[ds(g, 1)].squeeze(0)).then_inc(w_in[p], 16)

                ticks(sp, E0, [(0, load)])

            @block.tensor
            def _(pe):
                def up(g, p, j2):
                    pe.wait_ge(w_in[p], j2 * 32 + 32)
                    wait(pe, h_ready, g - 1)
                    for i in range(2):
                        last = nc.tensor.matmul(p_h[p][i][:], w1[p][:], flat[:, ds(g, 1), i * N:(i + 1) * N].rearrange("p a b -> p (a b)"), start=True, stop=True)
                    last.then_inc(up_done, 1)

                def down(g, p, j2):
                    pe.wait_ge(h_ready, g + 1)
                    wait(pe, y_kept, g - 1)
                    for i in range(2):
                        last = nc.tensor.matmul(p_y[p][i][:], w2[p][:], ht[p][:, i, :], start=True, stop=True)
                    last.then_inc(down_done, 1)

                ticks(pe, E0, [(0, up), (1, down)])

            @block.scalar
            def _(act):
                act.wait_ge(b_in, 32)

                def gelu(g, p, j2):
                    act.wait_ge(up_done, g + 1)
                    wait(act, down_done, g - 1)
                    for i in range(2):
                        last = nc.scalar.activation(ht[p][:, i, :], p_h[p][i][:], ACT.Gelu_apprx_tanh, bias=b1[:, ds(g, 1)])
                    last.then_inc(h_ready, 1)

                ticks(act, E0, [(0, gelu)])

            @block.vector
            def _(dve):
                dve.wait_ge(b_in, 32)

                def keep(g, p, j2):
                    dve.wait_ge(down_done, g + 1)
                    for i in range(2):
                        last = nc.vector.tensor_scalar(flat[:, ds(g, 1), i * N:(i + 1) * N].rearrange("p a b -> p (a b)"), p_y[p][i][:], b2[:, ds(g, 1)], None, ALU.add)
                    last.then_inc(y_kept, 1)

                ticks(dve, E0, [(0, keep)])


def gather_experts(nc, io, st):
    h, ident, xg, selt = st["h"], st["ident"], st["xg"], st["selt"]
    with ExitStack() as ctx:
        m = Mem(nc, ctx)
        xs = [m.sb(f"g_xs{i}", [D, TI, K0 * E0]) for i in range(2)]
        ss = [m.sb(f"g_ss{i}", [128, TI, S]) for i in range(2)]
        ys = m.sb("g_ys", [128, TI, D])
        p_y = [m.ps(f"g_py{i}", [128, G, D]) for i in range(2)]
        p_o = [m.ps(f"g_po{i}", [S, G, D]) for i in range(2)]
        xs_ready, ss_ready, y_turned, y_kept = m.sem("g_xs_ready"), m.sem("g_ss_ready"), m.sem("g_y_turned"), m.sem("g_y_kept")
        scattered, added, stats_made = m.sem("g_scattered"), m.sem("g_added"), m.sem("g_stats_made")
        NT = B // TI
        with nc.Block() as block:

            @block.scalar
            def _(act):
                def arrange(g, p, j2):
                    wait(act, y_turned, g - 1)
                    nc.scalar.copy(xs[p][:].rearrange("p a (k e) -> p a k e", k=K0),
                                   xg[:, :, ds(g * TI, TI), :].rearrange("p e a k -> p a k e")).then_inc(xs_ready, 1)

                def keep_y(g, p, j2):
                    act.wait_ge(y_turned, g + 1)
                    wait(act, scattered, g)
                    for i in range(2):
                        last = nc.scalar.copy(ys[:, i * G:(i + 1) * G, :], p_y[i][:])
                    last.then_inc(y_kept, 1)

                ticks(act, NT, [(0, arrange), (1, keep_y)])

            @block.vector
            def _(dve):
                def stage(g, p, j2):
                    wait(dve, scattered, g - 1)
                    nc.vector.tensor_copy(ss[p][:], selt[:, ds(g * TI, TI), :]).then_inc(ss_ready, 1)

                def add(g, p, j2):
                    dve.wait_ge(scattered, g + 1)
                    for i in range(2):
                        hs = h[:, ds(g * TI + i * G, G), :]
                        last = nc.vector.tensor_tensor(hs, hs, p_o[i][:], ALU.add)
                    last.then_inc(added, 1)
                    dve.wait_ge(added, g + 1)
                    token_statistics(nc, st, g * TI, TI).then_inc(stats_made, 1)

                ticks(dve, NT, [(0, stage), (1, add)])

            @block.tensor
            def _(pe):
                def turn_y(g, p, j2):
                    pe.wait_ge(xs_ready, g + 1)
                    wait(pe, y_kept, g)
                    for j in range(TI):
                        last = nc.tensor.transpose(p_y[j // G][:, j % G, :], xs[p][:, j, :], ident[:])
                    last.then_inc(y_turned, 1)

                def scatter(g, p, j2):
                    pe.wait_ge(y_kept, g + 1)
                    pe.wait_ge(ss_ready, g + 1)
                    wait(pe, added, g)
                    for j in range(TI):
                        last = nc.tensor.matmul(p_o[j // G][:, j % G, :], ss[p][:, j, :], ys[:, j, :], start=True, stop=True)
                    last.then_inc(scattered, 1)

                ticks(pe, NT, [(0, turn_y), (0, scatter)])


def expert_choice(nc, io, st):
    with ExitStack() as ctx:
        m = Mem(nc, ctx)
        st = dict(st, xg=m.sb("xg", [D, E0, B, K0]), selt=m.sb("selt", [128, B, S]))
        route_to_experts(nc, io, st)
        expert_layers(nc, io, st)
        gather_experts(nc, io, st)

def upto(n, most):
    return min(n, most) if isinstance(n, int) else n


def retention(nc, io, st):
    h, ident = st["h"], st["ident"]
    with ExitStack() as ctx:
        m = Mem(nc, ctx)
        names = ("wq1", "wq1_turn", "wk1", "wk1_turn", "wv1", "wg1", "wo1")
        wt = {n: m.sb(n, [D, D]) for n in names}
        tabs = {n: m.sb(n, [D, S]) for n in ("cos_q", "sin_q", "cos_k", "sin_k")}
        decay = m.sb("decay", [S, 2, NH // 2, S])
        mask, gnw, gnb = m.sb("head_mask", [D, 2]), m.sb("gnw", [D, 1]), m.sb("gnb", [D, 1])
        xn = [m.sb(f"t_xn{i}", [S, G, D]) for i in range(2)]
        xt = [m.sb(f"t_xt{i}", [D, W]) for i in range(2)]
        qc, qs, kc, ks, kt = (m.sb(f"t_{n}", [D, W]) for n in ("qc", "qs", "kc", "ks", "kt"))
        qt = [m.sb(f"t_qt{i}", [D, W]) for i in range(2)]
        km = [m.sb(f"t_km{i}", [D, G, NH, S]) for i in range(2)]
        v = [m.sb(f"t_v{i}", [S, G, D]) for i in range(2)]
        th = m.sb("t_th", [D, W])
        swish = m.sb("t_swish", [D, NG, W])
        neg = [m.sb(f"t_neg{i}", [S, 2, NH // 2]) for i in range(2)]
        lg, pt = ([m.sb(f"t_{n}{i}", [S, 2, NH // 2, S]) for i in range(2)] for n in ("lg", "pt"))
        ex, pd = ([m.sb(f"t_{n}{i}", [S, 2, NH // 2, S]) for i in range(G)] for n in ("ex", "pd"))
        tot = [m.sb(f"t_tot{i}", [S, G, NH]) for i in range(2)]
        inv, mu, ss, ve, rs = (m.sb(f"t_{n}", [S, G * NH]) for n in ("inv", "mu", "ss", "ve", "rs"))
        y, yc, sq, yh = (m.sb(f"t_{n}", [S, G * NH, DH]) for n in ("y", "yc", "sq", "yh"))
        u1, u = m.sb("t_u1", [D, W]), m.sb("t_u", [D, W])
        pm0, pm1, pm2, p_y = (m.ps(n, [128, 512]) for n in ("t_pm0", "t_pm1", "t_pm2", "t_py"))
        p_s, p_t = m.ps("t_ps", [S, 2, 512]), m.ps("t_pt", [S, 2, 512])
        scores = p_s[:, :, 0:W].rearrange("p a (b c) -> p a b c", c=S)
        turned = p_t[:, :, 0:W].rearrange("p a (b c) -> p a b c", c=S)
        ln = ln_statistics(nc, st, m, "t")
        sems = ("weights_in", "km_zeroed", "normed", "x_turned", "x_ready", "q_made", "q_read", "q_ready", "k_made", "k_read", "kt_ready",
                "km_ready", "v_made", "v_ready", "g_made", "tanh_ready", "swish_ready", "scored", "maxed",
                "shifted", "exped", "summed", "decayed", "p_turned", "pt_kept", "mixed", "inv_ready", "y_ready", "mu_ready",
                "yc_ready", "sq_ready", "ss_ready", "ve_ready", "rs_ready", "yh_ready", "y_turned", "u1_ready", "u_ready", "out_made",
                "added", "stats_made")
        s = {n: m.sem("t_" + n) for n in sems}
        n_in = 16 * (len(names) + 4 + 4)

        def images(t, a=G):
            return t.rearrange("p (a b) -> p a b", a=a)

        with nc.Block() as block:

            @block.sync
            def _(sp):
                for n in names:
                    sp.dma_start(wt[n][:], io[n]).then_inc(s["weights_in"], 16)
                for n in tabs:
                    sp.dma_start(tabs[n][:], io[n]).then_inc(s["weights_in"], 16)
                sp.dma_start(decay[:], io["decay"]).then_inc(s["weights_in"], 16)
                sp.dma_start(mask[:], io["head_mask"]).then_inc(s["weights_in"], 16)
                sp.dma_start(gnw[:], io["gnw"].unsqueeze(1)).then_inc(s["weights_in"], 16)
                sp.dma_start(gnb[:], io["gnb"].unsqueeze(1)).then_inc(s["weights_in"], 16)

            @block.vector
            def _(dve):
                ln_on_dve(nc, dve, ln)
                dve.wait_ge(s["weights_in"], n_in)

                def norm(g, p, j2):
                    wait(dve, s["x_turned"], g - 1)
                    normalise(nc, xn[p], st, g * G, G).then_inc(s["normed"], 1)

                def rotate_q(g, p, j2):
                    dve.wait_ge(s["q_made"], g + 1)
                    wait(dve, s["q_ready"], g)
                    nc.vector.tensor_tensor(images(qc[:]), images(pm1[:, 0:W]), bc(tabs["cos_q"][:], 1, G), ALU.mult)
                    nc.vector.tensor_tensor(images(qs[:]), images(pm2[:, 0:W]), bc(tabs["sin_q"][:], 1, G), ALU.mult).then_inc(s["q_read"], 1)

                def rotate_k(g, p, j2):
                    dve.wait_ge(s["k_made"], g + 1)
                    wait(dve, s["kt_ready"], g)
                    nc.vector.tensor_tensor(images(kc[:]), images(pm1[:, 0:W]), bc(tabs["cos_k"][:], 1, G), ALU.mult)
                    nc.vector.tensor_tensor(images(ks[:]), images(pm2[:, 0:W]), bc(tabs["sin_k"][:], 1, G), ALU.mult).then_inc(s["k_read"], 1)

                def gate(g, p, j2):
                    dve.wait_ge(s["tanh_ready"], g + 1)
                    nc.vector.scalar_tensor_tensor(out=swish[:, ds(g, 1), :].rearrange("p a b -> p (a b)"), in0=th[:], scalar=1.0, in1=pm2[:, 0:W],
                                                   op0=ALU.add, op1=ALU.mult).then_inc(s["swish_ready"], 1)

                def shift(j):
                    def step(g, p, j2):
                        n, q = g * G + j, j % 2
                        dve.wait_ge(s["scored"], n + 1)
                        nc.vector.tensor_reduce(neg[q][:], scores, X, ALU.max, negate=True).then_inc(s["maxed"], 1)
                        dve.wait_ge(s["maxed"], n + 1)
                        wait(dve, s["exped"], n - 1)
                        nc.vector.tensor_tensor(lg[q][:], scores, bc(neg[q][:], 3, S), ALU.add).then_inc(s["shifted"], 1)
                    return step

                def total(j):
                    def step(g, p, j2):
                        n, q = g * G + j, j % 2
                        dve.wait_ge(s["exped"], n + 1)
                        if j == 0:
                            wait(dve, s["inv_ready"], g - 1)
                        nc.vector.tensor_reduce(tot[p][:, j, :].rearrange("p (a b) -> p a b", a=2), ex[j][:], X, ALU.add).then_inc(s["summed"], 1)
                    return step

                def center(g, p, j2):
                    dve.wait_ge(s["summed"], g * G + G)
                    wait(dve, s["y_ready"], g)
                    nc.vector.reciprocal(inv[:], tot[p][:].rearrange("p a b -> p (a b)")).then_inc(s["inv_ready"], 1)
                    dve.wait_ge(s["inv_ready"], g + 1)
                    dve.wait_ge(s["mixed"], g * G + G)
                    nc.vector.tensor_tensor(y[:], p_y[0:S, :].rearrange("p (a b) -> p a b", b=DH), bc(inv[:], 2, DH), ALU.mult).then_inc(s["y_ready"], 1)
                    dve.wait_ge(s["y_ready"], g + 1)
                    nc.vector.tensor_reduce(mu[:], y[:], X, ALU.add).then_inc(s["mu_ready"], 1)
                    dve.wait_ge(s["mu_ready"], g + 1)
                    nc.vector.scalar_tensor_tensor(out=yc[:], in0=bc(mu[:], 2, DH), scalar=-1.0 / DH, in1=y[:], op0=ALU.mult,
                                                   op1=ALU.add).then_inc(s["yc_ready"], 1)

                def variance(g, p, j2):
                    dve.wait_ge(s["sq_ready"], g + 1)
                    nc.vector.tensor_reduce(ss[:], sq[:], X, ALU.add).then_inc(s["ss_ready"], 1)
                    dve.wait_ge(s["ss_ready"], g + 1)
                    nc.vector.tensor_scalar(ve[:], ss[:], 1.0 / DH, EPS, ALU.mult, ALU.add).then_inc(s["ve_ready"], 1)

                def head_norm(g, p, j2):
                    dve.wait_ge(s["rs_ready"], 2 * g + 2)
                    wait(dve, s["y_turned"], g)
                    nc.vector.tensor_tensor(yh[:], yc[:], bc(rs[:], 2, DH), ALU.mult).then_inc(s["yh_ready"], 1)

                def affine(g, p, j2):
                    dve.wait_ge(s["y_turned"], g + 1)
                    nc.vector.tensor_scalar(u1[:], pm0[:, 0:W], gnw[:, 0:1], gnb[:, 0:1], ALU.mult, ALU.add).then_inc(s["u1_ready"], 1)
                    dve.wait_ge(s["u1_ready"], g + 1)
                    wait(dve, s["out_made"], g)
                    nc.vector.scalar_tensor_tensor(out=u[:], in0=u1[:], scalar=0.5, in1=swish[:, ds(g, 1), :].rearrange("p a b -> p (a b)"),
                                                   op0=ALU.mult, op1=ALU.mult).then_inc(s["u_ready"], 1)

                def add(g, p, j2):
                    dve.wait_ge(s["out_made"], g + 1)
                    hs = h[:, ds(g * G, G), :]
                    nc.vector.tensor_tensor(hs, hs, pm0[0:S, :].rearrange("p (a b) -> p a b", a=G), ALU.add).then_inc(s["added"], 1)

                def statistics(g, p, j2):
                    dve.wait_ge(s["added"], g + 1)
                    token_statistics(nc, st, g * G, G).then_inc(s["stats_made"], 1)

                ticks(dve, NG, [
                    (3, shift(0)), (4, total(3)), (2, rotate_q), (7, statistics),
                    (3, shift(1)), (3, total(0)), (2, rotate_k), (5, variance), (0, norm),
                    (3, shift(2)), (3, total(1)), (6, affine), (5, head_norm),
                    (3, shift(3)), (3, total(2)), (2, gate), (6, add), (4, center)])

            @block.gpsimd
            def _(pool):
                for p in range(2):
                    nc.gpsimd.memset(km[p][:], 0.0).then_inc(s["km_zeroed"], 1)
                pool.wait_ge(s["weights_in"], n_in)

                def add_q(g, p, j2):
                    pool.wait_ge(s["q_read"], g + 1)
                    wait(pool, s["scored"], (g - 1) * G)
                    nc.gpsimd.tensor_tensor(qt[p][:], qc[:], qs[:], ALU.add).then_inc(s["q_ready"], 1)

                def add_k(g, p, j2):
                    pool.wait_ge(s["k_read"], g + 1)
                    wait(pool, s["km_ready"], 2 * g)
                    nc.gpsimd.tensor_tensor(kt[:], kc[:], ks[:], ALU.add).then_inc(s["kt_ready"], 1)

                def fade(j):
                    def step(g, p, j2):
                        n, q = g * G + j, j % 2
                        pool.wait_ge(s["exped"], n + 1)
                        wait(pool, s["p_turned"], n - 3)
                        nc.gpsimd.tensor_tensor(pd[j][:], ex[j][:], decay[:], ALU.mult).then_inc(s["decayed"], 1)
                    return step

                def power(part):
                    c = slice(part * G * NH // 2, (part + 1) * G * NH // 2)

                    def step(g, p, j2):
                        pool.wait_ge(s["ve_ready"], g + 1)
                        wait(pool, s["yh_ready"], g)
                        nc.gpsimd.tensor_tensor(rs[:, c], ve[:, c], st["minus_half"][:, c], ALU.pow).then_inc(s["rs_ready"], 1)
                    return step

                ticks(pool, NG, [(3, fade(3)), (1, add_q), (2, fade(0)), (1, add_k), (4, power(0)), (2, fade(1)), (4, power(1)), (2, fade(2))])

            @block.scalar
            def _(act):
                act.wait_ge(s["weights_in"], n_in)
                act.wait_ge(s["km_zeroed"], 2)

                def keep_x(g, p, j2):
                    act.wait_ge(s["x_turned"], g + 1)
                    wait(act, s["g_made"], g - 1)
                    nc.scalar.copy(xt[p][:], pm0[:, 0:W]).then_inc(s["x_ready"], 1)

                def mask_k(part):
                    def step(g, p, j2):
                        act.wait_ge(s["kt_ready"], g + 1)
                        wait(act, s["scored"], (g - 1) * G)
                        for q in (2 * part, 2 * part + 1):
                            rows = slice(32 * q, 32 * q + 32)
                            for i in range(2):
                                last = nc.scalar.activation(km[p][rows, :, 2 * q + i, :], images(kt[rows, :]), ACT.Copy, scale=mask[rows, i:i + 1])
                        last.then_inc(s["km_ready"], 1)
                    return step

                def keep_v(g, p, j2):
                    act.wait_ge(s["v_made"], g + 1)
                    wait(act, s["mixed"], (g - 1) * G)
                    nc.scalar.copy(v[p][:], images(pm1[0:S, :])).then_inc(s["v_ready"], 1)

                def gate_tanh(g, p, j2):
                    act.wait_ge(s["g_made"], g + 1)
                    wait(act, s["swish_ready"], g)
                    nc.scalar.activation(th[:], pm2[:, 0:W], ACT.Tanh, scale=0.5).then_inc(s["tanh_ready"], 1)

                def exponent(j):
                    def step(g, p, j2):
                        n, q = g * G + j, j % 2
                        act.wait_ge(s["shifted"], n + 1)
                        wait(act, s["summed"], n - 3)
                        wait(act, s["decayed"], n - 3)
                        nc.scalar.activation(ex[j][:], lg[q][:], ACT.Exp).then_inc(s["exped"], 1)
                    return step

                def keep_pt(j):
                    def step(g, p, j2):
                        n, q = g * G + j, j % 2
                        act.wait_ge(s["p_turned"], n + 1)
                        wait(act, s["mixed"], n - 1)
                        nc.scalar.copy(pt[q][:], turned).then_inc(s["pt_kept"], 1)
                    return step

                def square(g, p, j2):
                    act.wait_ge(s["yc_ready"], g + 1)
                    wait(act, s["ss_ready"], g)
                    nc.scalar.activation(sq[:], yc[:], ACT.Square).then_inc(s["sq_ready"], 1)

                ticks(act, NG, [
                    (3, keep_pt(1)), (2, exponent(0)), (4, square),
                    (3, keep_pt(2)), (2, exponent(1)), (1, mask_k(0)),
                    (3, keep_pt(3)), (2, exponent(2)), (1, mask_k(1)), (1, keep_v), (1, gate_tanh),
                    (2, keep_pt(0)), (2, exponent(3)), (0, keep_x)])

            @block.tensor
            def _(pe):
                pe.wait_ge(s["weights_in"], n_in)

                def turn_x(g, p, j2):
                    pe.wait_ge(s["normed"], g + 1)
                    wait(pe, s["x_ready"], g)
                    wait(pe, s["added"], g - 4)
                    for j in range(G):
                        last = nc.tensor.transpose(pm0[:, j * S:(j + 1) * S], xn[p][:, j, :], ident[0:S, 0:S])
                    last.then_inc(s["x_turned"], 1)

                def make_q(g, p, j2):
                    pe.wait_ge(s["x_ready"], g + 1)
                    wait(pe, s["v_ready"], g)
                    wait(pe, s["swish_ready"], g)
                    nc.tensor.matmul(pm1[:, 0:W], wt["wq1"][:], xt[p][:], start=True, stop=True)
                    nc.tensor.matmul(pm2[:, 0:W], wt["wq1_turn"][:], xt[p][:], start=True, stop=True).then_inc(s["q_made"], 1)

                def make_k(g, p, j2):
                    pe.wait_ge(s["q_read"], g + 1)
                    nc.tensor.matmul(pm1[:, 0:W], wt["wk1"][:], xt[p][:], start=True, stop=True)
                    nc.tensor.matmul(pm2[:, 0:W], wt["wk1_turn"][:], xt[p][:], start=True, stop=True).then_inc(s["k_made"], 1)

                def make_v(g, p, j2):
                    pe.wait_ge(s["k_read"], g + 1)
                    for j in range(G):
                        last = nc.tensor.matmul(pm1[0:S, j * D:(j + 1) * D], xt[p][:, j * S:(j + 1) * S], wt["wv1"][:], start=True, stop=True)
                    last.then_inc(s["v_made"], 1)
                    nc.tensor.matmul(pm2[:, 0:W], wt["wg1"][:], xt[p][:], start=True, stop=True).then_inc(s["g_made"], 1)

                def score(j):
                    def step(g, p, j2):
                        n = g * G + j
                        if j == 0:
                            pe.wait_ge(s["q_ready"], g + 1)
                            pe.wait_ge(s["km_ready"], 2 * g + 2)
                        wait(pe, s["shifted"], n)
                        for i in range(2):
                            last = nc.tensor.matmul(p_s[:, i, 0:W], qt[p][:, j * S:(j + 1) * S],
                                                    km[p][:, j, i * 4:i * 4 + 4, :].rearrange("p a b -> p (a b)"), start=True, stop=True)
                        last.then_inc(s["scored"], 1)
                    return step

                def turn_p(j):
                    def step(g, p, j2):
                        n, q = g * G + j, j % 2
                        pe.wait_ge(s["decayed"], n + 1)
                        wait(pe, s["pt_kept"], n)
                        for i in range(NH):
                            last = nc.tensor.transpose(turned[:, i // 4, i % 4, :], pd[j][:, i // 4, i % 4, :], ident[0:S, 0:S])
                        last.then_inc(s["p_turned"], 1)
                    return step

                def mix(j):
                    def step(g, p, j2):
                        n, q = g * G + j, j % 2
                        pe.wait_ge(s["pt_kept"], n + 1)
                        if j == 0:
                            pe.wait_ge(s["v_ready"], g + 1)
                            wait(pe, s["y_ready"], g)
                        for i in range(NH):
                            c = j * D + i * DH
                            last = nc.tensor.matmul(p_y[0:S, c:c + DH], pt[q][:, i // 4, i % 4, :], v[p][:, j, i * DH:(i + 1) * DH], start=True, stop=True)
                        last.then_inc(s["mixed"], 1)
                    return step

                def turn_y(g, p, j2):
                    pe.wait_ge(s["yh_ready"], g + 1)
                    wait(pe, s["x_ready"], upto(g + 5, NG))
                    wait(pe, s["added"], g)
                    for j in range(G):
                        last = nc.tensor.transpose(pm0[:, j * S:(j + 1) * S], yh[:, j * NH:(j + 1) * NH, :].rearrange("p a b -> p (a b)"), ident[0:S, 0:S])
                    last.then_inc(s["y_turned"], 1)

                def out(g, p, j2):
                    pe.wait_ge(s["u_ready"], g + 1)
                    for j in range(G):
                        last = nc.tensor.matmul(pm0[0:S, j * D:(j + 1) * D], u[:, j * S:(j + 1) * S], wt["wo1"][:], start=True, stop=True)
                    last.then_inc(s["out_made"], 1)

                ticks(pe, NG, [
                    (2, score(0)), (1, make_q), (3, turn_p(1)), (3, mix(0)), (5, turn_y),
                    (2, score(1)), (1, make_k), (3, turn_p(2)), (3, mix(1)),
                    (2, score(2)), (1, make_v), (3, turn_p(3)), (3, mix(2)), (5, out),
                    (2, score(3)), (2, turn_p(0)), (3, mix(3)), (0, turn_x)])

def top2_gates(nc, io, st):
    ident, xt_all, comb = st["ident"], st["xt_all"], st["comb"]
    with ExitStack() as ctx:
        m = Mem(nc, ctx)
        wr, br = m.sb("m_wr", [D, E1]), m.sb("m_br", [S, E1])
        xn = [m.sb(f"m_xn{i}", [S, G, D]) for i in range(2)]
        xt = [m.sb(f"m_xt{i}", [D, W]) for i in range(2)]
        lg, ex, prob, rank = (m.sb(f"m_{n}", [S, B, E1]) for n in ("lg", "ex", "prob", "rank"))
        neg, inv = m.sb("m_neg", [S, B]), m.sb("m_inv", [S, B])
        beats = m.sb("m_beats", [S, B, E1, E1])
        p_x = [m.ps(f"m_px{i}", [D, W]) for i in range(2)]
        p_l = [m.ps(f"m_pl{i}", [S, G, E1]) for i in range(2)]
        ln = ln_statistics(nc, st, m, "m")
        w_in, zeroed = m.sem("m_weights_in"), m.sem("m_beats_zeroed")
        normed, x_turned, x_ready, x_kept = m.sem("m_normed"), m.sem("m_x_turned"), m.sem("m_x_ready"), m.sem("m_x_kept")
        gated, logits_kept, exped, chain = m.sem("m_gated"), m.sem("m_logits_kept"), m.sem("m_exped"), m.sem("m_chain")
        with nc.Block() as block:

            @block.sync
            def _(sp):
                sp.dma_start(wr[:], io["wr_t"]).then_inc(w_in, 16)
                sp.dma_start(br[:], row_broadcast(io["br"], S)).then_inc(w_in, 16)

            @block.gpsimd
            def _(pool):
                nc.gpsimd.memset(beats[:], 0.0).then_inc(zeroed, 1)

            @block.vector
            def _(dve):
                ln_on_dve(nc, dve, ln)
                dve.wait_ge(w_in, 32)

                def norm(g, p, j2):
                    wait(dve, x_turned, g - 1)
                    normalise(nc, xn[p], st, g * G, G).then_inc(normed, 1)

                def keep_logits(g, p, j2):
                    dve.wait_ge(gated, g + 1)
                    nc.vector.tensor_tensor(lg[:, ds(g * G, G), :], p_l[p][:], bc(br[:], 1, G), ALU.add).then_inc(logits_kept, 1)

                ticks(dve, NG, [(2, keep_logits), (0, norm)])

                done = 0

                def then(ins):
                    nonlocal done
                    ins.then_inc(chain, 1)
                    done += 1
                    dve.wait_ge(chain, done)

                dve.wait_ge(logits_kept, NG)
                then(nc.vector.tensor_reduce(neg[:], lg[:], X, ALU.max, negate=True))
                then(nc.vector.tensor_tensor(lg[:], lg[:], bc(neg[:], 2, E1), ALU.add))
                dve.wait_ge(exped, 1)
                then(nc.vector.tensor_reduce(neg[:], ex[:], X, ALU.add))
                then(nc.vector.reciprocal(inv[:], neg[:]))
                then(nc.vector.tensor_tensor(prob[:], ex[:], bc(inv[:], 2, E1), ALU.mult))
                dve.wait_ge(zeroed, 1)
                for e in range(E1):
                    if e > 0:
                        last = nc.vector.tensor_tensor(beats[:, :, e, 0:e], prob[:, :, 0:e], bc(prob[:, :, e], 2, e), ALU.is_ge)
                    if e < E1 - 1:
                        last = nc.vector.tensor_tensor(beats[:, :, e, e + 1:E1], prob[:, :, e + 1:E1], bc(prob[:, :, e], 2, E1 - 1 - e), ALU.is_gt)
                then(last)
                then(nc.vector.tensor_reduce(rank[:], beats[:], X, ALU.add))
                then(nc.vector.scalar_tensor_tensor(out=ex[:], in0=rank[:], scalar=1.5, in1=prob[:], op0=ALU.is_lt, op1=ALU.mult))
                then(nc.vector.tensor_copy(comb[:, :, 0, :], ex[:]))
                then(nc.vector.tensor_tensor(prob[:], ex[:], comb[:, :, 0, :], ALU.subtract))
                then(nc.vector.tensor_copy(comb[:, :, 1, :], prob[:]))
                then(nc.vector.tensor_tensor(rank[:], prob[:], comb[:, :, 1, :], ALU.subtract))
                then(nc.vector.tensor_copy(comb[:, :, 2, :], rank[:]))

            @block.scalar
            def _(act):
                def keep_x(g, p, j2):
                    act.wait_ge(x_turned, g + 1)
                    wait(act, gated, g - 1)
                    nc.scalar.copy(xt[p][:], p_x[p][:]).then_inc(x_ready, 1)
                    nc.scalar.copy(xt_all[:, ds(g * G, G), :], p_x[p][:].rearrange("p (a b) -> p a b", a=G)).then_inc(x_kept, 1)

                ticks(act, NG, [(0, keep_x)])
                act.wait_ge(chain, 2)
                nc.scalar.activation(ex[:], lg[:], ACT.Exp).then_inc(exped, 1)

            @block.tensor
            def _(pe):
                pe.wait_ge(w_in, 32)

                def turn_x(g, p, j2):
                    pe.wait_ge(normed, g + 1)
                    wait(pe, x_kept, g - 1)
                    for j in range(G):
                        last = nc.tensor.transpose(p_x[p][:, j * S:(j + 1) * S], xn[p][:, j, :], ident[0:S, 0:S])
                    last.then_inc(x_turned, 1)

                def gates(g, p, j2):
                    pe.wait_ge(x_ready, g + 1)
                    wait(pe, logits_kept, g - 1)
                    for j in range(G):
                        last = nc.tensor.matmul(p_l[p][:, j, :], xt[p][:, j * S:(j + 1) * S], wr[:], start=True, stop=True)
                    last.then_inc(gated, 1)

                ticks(pe, NG, [(0, turn_x), (1, gates)])


def top2_layers(nc, io, st):
    h, ident, xt_all, comb = st["h"], st["ident"], st["xt_all"], st["comb"]
    NI = E1 * (H1 // D)
    ROWS = 3 * E1
    with ExitStack() as ctx:
        m = Mem(nc, ctx)
        w1, w2 = m.sb("n_w1", [D, E1, H1]), m.sb("n_w2", [D, NI, D])
        b1 = m.sb("n_b1", [D, NI])
        b2f, b2r = m.sb("n_b2f", [ROWS, D]), m.sb("n_b2r", [ROWS, D])
        b2 = [m.sb(f"n_b2_{i}", [ROWS, D], BF16) for i in range(3)]
        pickf, pick = m.sb("n_pickf", [ROWS, E1, D]), m.sb("n_pick", [ROWS, E1, D], BF16)
        identb = m.sb("n_identb", [S, S], BF16)
        cs = [m.sb(f"n_cs{i}", [S, G, ROWS], BF16) for i in range(2)]
        ct = [m.sb(f"n_ct{i}", [ROWS, W], BF16) for i in range(2)]
        hg = [m.sb(f"n_hg{i}", [D, W]) for i in range(2)]
        hs = [m.sb(f"n_hs{i}", [D, W]) for i in range(4)]
        yt = [m.sb(f"n_yt{i}", [D, W]) for i in range(2)]
        ho = [m.sb(f"n_ho{i}", [S, G, D]) for i in range(2)]
        p_h = [m.ps(f"n_ph{i}", [D, W]) for i in range(2)]
        p_b = [m.ps(f"n_pb{i}", [D, W]) for i in range(2)]
        p_y = [m.ps(f"n_py{i}", [D, W]) for i in range(2)]
        p_c, p_o = m.ps("n_pc", [ROWS, G, S + 1], BF16), m.ps("n_po", [S, G, D])
        sems = ("weights_in", "b2_split", "consts_ready", "cs_ready", "c_turned", "ct_ready", "hidden", "gate_spread", "gelu_done",
                "scaled", "multiplied", "y_done", "yt_ready", "y_turned", "sum_ready")
        s = {n: m.sem("n_" + n) for n in sems}
        stored = [m.sem(f"n_stored{i}") for i in range(2)]
        n_in = 16 * 7
        with nc.Block() as block:

            @block.sync
            def _(sp):
                sp.dma_start(w1[:], io["W1"].rearrange("e d h -> d e h")).then_inc(s["weights_in"], 16)
                sp.dma_start(w2[:], io["W2"].rearrange("e (c p) d -> p (e c) d", p=D)).then_inc(s["weights_in"], 16)
                sp.dma_start(b1[:], io["b1m_t"]).then_inc(s["weights_in"], 16)
                sp.dma_start(pickf[:], io["pick"]).then_inc(s["weights_in"], 16)
                for i in range(3):
                    sp.dma_start(b2f[i * E1:(i + 1) * E1, :], io["b2m"]).then_inc(s["weights_in"], 16)

                def put(g, p, j2):
                    sp.wait_ge(s["sum_ready"], g + 1)
                    sp.dma_start(io["out"][ds(g * G, G)].rearrange("b s d -> s b d"), ho[p][:]).then_inc(stored[p], 16)

                ticks(sp, NG, [(0, put)])
                for p in range(2):
                    sp.wait_ge(stored[p], NG // 2 * 16)

            @block.gpsimd
            def _(pool):
                def stage(g, p, j2):
                    wait(pool, s["c_turned"], g - 1)
                    nc.gpsimd.tensor_copy(cs[p][:], comb[:, ds(g * G, G), :, :].rearrange("p a b c -> p a (b c)")).then_inc(s["cs_ready"], 1)

                ticks(pool, NG, [(0, stage)])

            @block.vector
            def _(dve):
                dve.wait_ge(s["weights_in"], n_in)
                nc.vector.tensor_copy(identb[:], ident[0:S, 0:S])
                nc.vector.tensor_copy(pick[:], pickf[:])
                nc.vector.tensor_copy(b2[0][:], b2f[:]).then_inc(s["b2_split"], 1)
                dve.wait_ge(s["b2_split"], 1)
                nc.vector.tensor_tensor(b2r[:], b2f[:], b2[0][:], ALU.subtract).then_inc(s["b2_split"], 1)
                dve.wait_ge(s["b2_split"], 2)
                nc.vector.tensor_copy(b2[1][:], b2r[:]).then_inc(s["b2_split"], 1)
                dve.wait_ge(s["b2_split"], 3)
                nc.vector.tensor_tensor(b2f[:], b2r[:], b2[1][:], ALU.subtract).then_inc(s["b2_split"], 1)
                dve.wait_ge(s["b2_split"], 4)
                nc.vector.tensor_copy(b2[2][:], b2f[:]).then_inc(s["consts_ready"], 1)

                def keep_gates(g, p, j2):
                    dve.wait_ge(s["c_turned"], g + 1)
                    wait(dve, s["y_done"], g - 1)
                    nc.vector.tensor_copy(ct[p][:].rearrange("p (a b) -> p a b", a=G), p_c[:, :, 0:S]).then_inc(s["ct_ready"], 1)

                def scale(i):
                    def step(g, p, j2):
                        n = g * NI + i
                        dve.wait_ge(s["gelu_done"], n + 1)
                        if i % 2 == 0:
                            dve.wait_ge(s["gate_spread"], g * E1 + i // 2 + 1)
                        wait(dve, s["multiplied"], n - 3)
                        nc.vector.tensor_tensor(hs[i % 4][:], hg[i % 2][:], p_b[i // 2 % 2][:], ALU.mult).then_inc(s["scaled"], 1)
                    return step

                def keep_y(g, p, j2):
                    dve.wait_ge(s["y_done"], g + 1)
                    wait(dve, s["y_turned"], g - 1)
                    nc.vector.tensor_copy(yt[p][:], p_y[p][:]).then_inc(s["yt_ready"], 1)

                def add(g, p, j2):
                    dve.wait_ge(s["y_turned"], g + 1)
                    wait(dve, stored[p], j2 * 16)
                    nc.vector.tensor_tensor(ho[p][:], h[:, ds(g * G, G), :], p_o[:], ALU.add).then_inc(s["sum_ready"], 1)

                ticks(dve, NG, [(1, scale(0)), (1, scale(1)), (2, keep_y)] + [(1, scale(i)) for i in range(2, 8)] + [(2, add), (0, keep_gates)]
                      + [(1, scale(i)) for i in range(8, NI)])

            @block.scalar
            def _(act):
                act.wait_ge(s["weights_in"], n_in)

                def gelu(i):
                    def step(g, p, j2):
                        n = g * NI + i
                        act.wait_ge(s["hidden"], n + 1)
                        wait(act, s["scaled"], n - 1)
                        nc.scalar.activation(hg[i % 2][:], p_h[i % 2][:], ACT.Gelu, bias=b1[:, i:i + 1]).then_inc(s["gelu_done"], 1)
                    return step

                ticks(act, NG, [(0, gelu(i)) for i in range(NI)])

            @block.tensor
            def _(pe):
                pe.wait_ge(s["weights_in"], n_in)
                pe.wait_ge(s["consts_ready"], 1)

                def turn_gates(g, p, j2):
                    pe.wait_ge(s["cs_ready"], g + 1)
                    wait(pe, s["ct_ready"], g)
                    for j in range(G):
                        last = nc.tensor.transpose(p_c[:, j, 0:S], cs[p][:, j, :], identb[:])
                    last.then_inc(s["c_turned"], 1)

                def up(i):
                    def step(g, p, j2):
                        n, e = g * NI + i, i // 2
                        if i == 0:
                            pe.wait_ge(s["ct_ready"], g + 1)
                        if i % 2 == 0:
                            wait(pe, s["scaled"], n - 2)
                            nc.tensor.matmul(p_b[e % 2][:], pick[:, e, :], ct[p][:], start=True, stop=True).then_inc(s["gate_spread"], 1)
                        wait(pe, s["gelu_done"], n - 1)
                        nc.tensor.matmul(p_h[i % 2][:], w1[:, e, i % 2 * D:(i % 2 + 1) * D], xt_all[:, ds(g * G, G), :].rearrange("p a b -> p (a b)"),
                                         start=True, stop=True).then_inc(s["hidden"], 1)
                    return step

                def down(i):
                    def step(g, p, j2):
                        n = g * NI + i
                        pe.wait_ge(s["scaled"], n + 1)
                        if i == 0:
                            wait(pe, s["yt_ready"], g - 1)
                        nc.tensor.matmul(p_y[p][:], w2[:, i, :], hs[i % 4][:], start=i == 0, stop=False).then_inc(s["multiplied"], 1)
                        if i == NI - 1:
                            for k in range(3):
                                last = nc.tensor.matmul(p_y[p][:], b2[k][:], ct[p][:], start=False, stop=k == 2)
                            last.then_inc(s["y_done"], 1)
                    return step

                def turn_y(g, p, j2):
                    pe.wait_ge(s["yt_ready"], g + 1)
                    wait(pe, s["sum_ready"], g)
                    for j in range(G):
                        last = nc.tensor.transpose(p_o[:, j, :], yt[p][:, j * S:(j + 1) * S], ident[:])
                    last.then_inc(s["y_turned"], 1)

                steps = []
                for i in range(NI):
                    steps.append((1, up(i)))
                    steps.append((2, down(NI - 2 + i)) if i < 2 else (1, down(i - 2)))
                    if i == 5:
                        steps.append((2, turn_y))
                    if i == 7:
                        steps.append((0, turn_gates))
                ticks(pe, NG, steps)


def top2_experts(nc, io, st):
    with ExitStack() as ctx:
        m = Mem(nc, ctx)
        st = dict(st, xt_all=m.sb("xt_all", [D, B, S]), comb=m.sb("comb", [S, B, 3, E1], BF16))
        top2_gates(nc, io, st)
        top2_layers(nc, io, st)


def tower(nc, io):
    with ExitStack() as ctx:
        m = Mem(nc, ctx)
        st = {
            "h": m.sb("h", [S, B, D]),
            "stats": m.sb("stats", [S, B, 6]),
            "ident": m.sb("ident", [128, 128]),
            "mean": m.sb("mean", [S, B]),
            "rstd": m.sb("rstd", [S, B]),
            "minus_half": m.sb("minus_half", [S, B]),
        }
        patch_tokens(nc, io, st)
        attention(nc, io, st)
        expert_choice(nc, io, st)
        retention(nc, io, st)
        top2_experts(nc, io, st)


def constants():
    f = np.float32
    pos = np.arange(S, dtype=f)[:, None]
    div = np.exp(np.arange(0, D, 2, dtype=f) * f(-np.log(10000.0) / D)).astype(f)
    ang = pos * div
    sinus_t = np.concatenate([np.sin(ang), np.cos(ang)], axis=-1).astype(f).T
    sv = (np.arange(0, DH, 2, dtype=f) + f(0.4 * DH)) / f(1.4 * DH)
    scale = (sv[None, :] ** (np.arange(S, dtype=f) / f(128))[:, None]).astype(f)
    ang1 = np.arange(S, dtype=f)[:, None] * (f(1) / f(10000) ** (np.arange(DH // 2, dtype=f) / f(DH // 2)))[None, :]
    sign = np.tile(np.array([-1, 1], f), D // 2)[:, None]
    tab = {}
    for n, sc in (("q", scale), ("k", f(1) / scale)):
        tab[f"cos_{n}"] = np.tile(np.repeat(np.cos(ang1) * sc, 2, axis=1), (1, NH)).T.astype(f)
        tab[f"sin_{n}"] = np.tile(np.repeat(np.sin(ang1) * sc, 2, axis=1), (1, NH)).T.astype(f) * sign
    gammas = (1 - np.exp(np.linspace(np.log(1 / 32), np.log(1 / 128), NH))).astype(f)
    dist = np.abs(np.arange(S)[:, None] - np.arange(S)[None, :]).astype(f)
    tab["decay"] = (gammas[None, :, None] ** dist[:, None, :]).astype(f).reshape(S, 2, NH // 2, S)
    tab["head_mask"] = np.stack([(np.arange(D) // DH % 2 == i) for i in range(2)], axis=1).astype(f)
    tab["pick"] = np.repeat(np.tile(np.eye(E1, dtype=f), (3, 1))[:, :, None], D, axis=2)
    return {**tab, "sinus_t": np.ascontiguousarray(sinus_t), "iota": np.arange(S, dtype=f)}


def heads(w):
    return w.transpose(1, 0, 2).reshape(D, D)


def kernel(**inputs):
    import concourse.bacc as bacc
    from concourse.bass_utils import run_bass_kernel_spmd

    a = {k: np.asarray(v) for k, v in inputs.items()}
    img = a["x"].reshape(B // TI, TI, 3, PY, PATCH, PY, PATCH)
    data = {
        "patches": img.transpose(0, 2, 4, 6, 1, 3, 5).reshape(B // TI, IN_D, TN),
        "tok_wt": a["L0_tok_W"].T,
        "pos_t": a["L0_tok_pos_embed"].T,
        "tok_b": a["L0_tok_b"],
        "cls_t": a["L0_tok_class_token"].T,
        "wq_t": a["L0_attn_Wq"].T, "wk_t": a["L0_attn_Wk"].T, "wv_t": a["L0_attn_Wv"].T,
        "gate": a["L0_ffn_gate_weight"], "w1": a["L0_ffn_w1"], "w2": a["L0_ffn_w2"], "b1_t": a["L0_ffn_b1"].T, "b2_t": a["L0_ffn_b2"].T,
        "bq": a["L0_attn_bq"], "bk": a["L0_attn_bk"], "bv": a["L0_attn_bv"],
        "wv1": heads(a["L1_attn_W_V"]), "wg1": a["L1_attn_W_G"], "wo1": a["L1_attn_W_O"],
        "gnw": a["L1_attn_gn_weight"], "gnb": a["L1_attn_gn_bias"],
    }
    data.update({
        "wr_t": a["L1_ffn_Wr"].T, "br": a["L1_ffn_br"], "W1": a["L1_ffn_W1"], "W2": a["L1_ffn_W2"],
        "b1m_t": a["L1_ffn_b1"].reshape(E1 * H1 // D, D).T, "b2m": a["L1_ffn_b2"],
    })
    for n in "qk":
        data[f"w{n}1"] = heads(a[f"L1_attn_W_{n.upper()}"])
        data[f"w{n}1_turn"] = data[f"w{n}1"].reshape(D, D // 2, 2)[:, :, ::-1].reshape(D, D)
    data.update(constants())
    nc = bacc.Bacc("TRN2", target_bir_lowering=False, num_devices=1)
    arrays, io = {}, {}
    for name, v in data.items():
        arrays[f"in_{name}"] = np.ascontiguousarray(v)
        io[name] = nc.dram_tensor(f"in_{name}", v.shape, mybir.dt.from_np(v.dtype), kind="ExternalInput").ap()
    io["out"] = nc.dram_tensor("out_0", (B, S, D), F32, kind="ExternalOutput").ap()
    tower(nc, io)
    return run_bass_kernel_spmd(nc, [arrays], core_ids=[0]).results[0]["out_0"]
```

```python
import numpy as np
import concourse.bass as bass
from concourse import mybir
from concourse.alu_op_type import AluOpType as ALU
from contextlib import ExitStack

F32 = mybir.dt.float32
F32R = mybir.dt.float32r
BF16 = mybir.dt.bfloat16
U32 = mybir.dt.uint32
I32 = mybir.dt.int32
ACT = mybir.ActivationFunctionType
X = mybir.AxisListType.X
ds = bass.ds

B = 128
PY = 8
NP = PY * PY
S = NP + 1
D = 128
PATCH = 28
IN_D = 3 * PATCH * PATCH
KC = 19
KP = -(-IN_D // KC)
KLAST = IN_D - (KP - 1) * KC
TI = 8
TN = TI * NP
G = 4
W = G * S
NG = B // G
E0, K0 = 16, 8
E1, H1 = 8, 256
NH, DH = 8, 16
EPS = 1e-5


def bc(ap, axis, n):
    shape = list(ap.shape)
    return ap.unsqueeze(axis).broadcast_to(shape[:axis] + [n] + shape[axis:])


def ticks(eng, count, steps):
    deep = max(k for k, _ in steps)
    head = (deep + 3) // 2 * 2
    for t in range(head):
        for k, step in steps:
            if t >= k:
                step(t - k, (t - k) % 2, (t - k) // 2)
    with eng.Fori(head // 2, count // 2) as i:
        for u in range(2):
            for k, step in steps:
                step(i * 2 + (u - k), (u - k) % 2, i + (u - k) // 2)
    for t in range(count, count + deep):
        for k, step in steps:
            if t - k < count:
                step(t - k, (t - k) % 2, (t - k) // 2)


def wait(eng, sem, n):
    if isinstance(n, int) and n <= 0:
        return
    eng.wait_ge(sem, n)


class Mem:

    def __init__(self, nc, ctx):
        self.nc, self.ctx = nc, ctx

    def sb(self, name, shape, dt=F32):
        return self.ctx.enter_context(self.nc.sbuf_tensor(name, shape, dt))

    def ps(self, name, shape, dt=F32):
        return self.ctx.enter_context(self.nc.psum_tensor(name, shape, dt))

    def sem(self, name):
        return self.ctx.enter_context(self.nc.semaphore(name))


def row_broadcast(dram_row, parts):
    return dram_row.unsqueeze(0).broadcast_to([parts, dram_row.shape[0]])


def patch_tokens(nc, io, st):
    h, stats, ident = st["h"], st["stats"], st["ident"]
    with ExitStack() as ctx:
        m = Mem(nc, ctx)
        w = m.sb("tok_w", [128, KC, D])
        x = [m.sb(f"tok_x{i}", [128, KC, TN]) for i in range(2)]
        tok_t = [m.sb(f"tok_t{i}", [D, TI, S]) for i in range(2)]
        pos_t, bias, cls = m.sb("pos_t", [D, S]), m.sb("tok_bias", [D, 1]), m.sb("tok_cls", [D, 1])
        p_emb = [m.ps(f"p_emb{i}", [D, TI, NP]) for i in range(2)]
        p_tok = [m.ps(f"p_tok{i}", [128, G, D]) for i in range(4)]
        consts_in, x_in = m.sem("tok_consts_in"), [m.sem(f"x_in{i}") for i in range(2)]
        ident0, ident_made = m.sem("ident_zeroed"), m.sem("ident_made")
        embedded, tok_made, cls_made = m.sem("embedded"), m.sem("tok_made"), m.sem("cls_made")
        turned, h_made, stats_made = m.sem("tok_turned"), m.sem("h_made"), m.sem("tok_stats_made")
        NT = B // TI
        with nc.Block() as block:

            @block.sync
            def _(sp):
                sp.dma_start(w[0:KP - 1], io["tok_wt"][0:(KP - 1) * KC, :].rearrange("(p c) n -> p c n", c=KC)).then_inc(consts_in, 16)
                sp.dma_start(w[KP - 1:KP, 0:KLAST], io["tok_wt"][(KP - 1) * KC:IN_D, :].unsqueeze(0)).then_inc(consts_in, 16)
                sp.dma_start(pos_t[:], io["pos_t"]).then_inc(consts_in, 16)
                sp.dma_start(bias[:], io["tok_b"].unsqueeze(1)).then_inc(consts_in, 16)
                sp.dma_start(cls[:], io["cls_t"]).then_inc(consts_in, 16)

                def load(g, p, j2):
                    wait(sp, embedded, g - 1)
                    blk = io["patches"][g] if isinstance(g, int) else io["patches"][ds(g, 1)].squeeze(0)
                    sp.dma_start(x[p][0:KP - 1], blk[0:(KP - 1) * KC, :].rearrange("(p c) n -> p c n", c=KC)).then_inc(x_in[p], 16)
                    sp.dma_start(x[p][KP - 1:KP, 0:KLAST], blk[(KP - 1) * KC:IN_D, :].unsqueeze(0)).then_inc(x_in[p], 16)

                ticks(sp, NT, [(0, load)])

            @block.gpsimd
            def _(pool):
                nc.gpsimd.memset(st["minus_half"][:], -0.5)
                nc.gpsimd.memset(ident[:], 0.0).then_inc(ident0, 1)
                pool.wait_ge(ident0, 1)
                nc.gpsimd.affine_select(out=ident[:], in_=ident[:], compare_op=ALU.not_equal, fill=1.0, base=0,
                                        pattern=[[-1, 128]], channel_multiplier=1).then_inc(ident_made, 1)

            @block.tensor
            def _(pe):
                pe.wait_ge(consts_in, 80)
                pe.wait_ge(ident_made, 1)

                def embed(g, p, j2):
                    pe.wait_ge(x_in[p], j2 * 32 + 32)
                    wait(pe, tok_made, g - 1)
                    for c in range(KC):
                        k = KP if c < KLAST else KP - 1
                        last = nc.tensor.matmul(p_emb[p][:], w[0:k, c, :], x[p][0:k, c, :], start=c == 0, stop=c == KC - 1)
                    last.then_inc(embedded, 1)

                def turn(g, p, j2):
                    pe.wait_ge(tok_made, g + 1)
                    wait(pe, h_made, g - 1)
                    for j in range(TI):
                        last = nc.tensor.transpose(p_tok[2 * p + j // G][0:S, j % G, :], tok_t[p][:, j, :], ident[:])
                    last.then_inc(turned, 1)

                ticks(pe, NT, [(0, embed), (1, turn)])

            @block.vector
            def _(dve):
                dve.wait_ge(consts_in, 80)
                for p in range(2):
                    nc.vector.tensor_tensor(tok_t[p][:, :, 0], bc(cls[:, 0], 1, TI), bc(pos_t[:, 0], 1, TI), ALU.mult).then_inc(cls_made, 1)

                def finish(g, p, j2):
                    dve.wait_ge(embedded, g + 1)
                    wait(dve, turned, g - 1)
                    nc.vector.scalar_tensor_tensor(out=tok_t[p][:, :, 1:S], in0=p_emb[p][:], scalar=bias[:, 0:1], in1=bc(pos_t[:, 1:S], 1, TI),
                                                   op0=ALU.add, op1=ALU.mult).then_inc(tok_made, 1)

                def statistics(g, p, j2):
                    dve.wait_ge(h_made, g + 1)
                    for j in range(TI):
                        last = nc.vector.bn_stats(stats[:, ds(g * TI + j, 1), :].rearrange("p a b -> p (a b)"),
                                                  h[:, ds(g * TI + j, 1), :].rearrange("p a b -> p (a b)"))
                    last.then_inc(stats_made, 1)

                ticks(dve, NT, [(0, finish), (2, statistics)])

            @block.scalar
            def _(act):
                def keep(g, p, j2):
                    act.wait_ge(turned, g + 1)
                    for i in range(2):
                        last = nc.scalar.copy(h[:, ds(g * TI + i * G, G), :], p_tok[2 * p + i][0:S])
                    last.then_inc(h_made, 1)

                ticks(act, NT, [(0, keep)])


def inverse_root(nc, dve, out, v, t, step, base):
    n = base

    def then(ins):
        nonlocal n
        ins.then_inc(step, 1)
        n = n + 1
        dve.wait_ge(step, n)

    then(nc.vector.tensor_scalar(t.bitcast(I32), v.bitcast(I32), 1, None, ALU.logical_shift_right))
    then(nc.vector.tensor_scalar(out.bitcast(I32), t.bitcast(I32), -1.0, float(0x5F3759DF), ALU.mult, ALU.add))
    for _ in range(3):
        then(nc.vector.tensor_tensor(t, out, out, ALU.mult))
        then(nc.vector.scalar_tensor_tensor(out=t, in0=t, scalar=-0.5, in1=v, op0=ALU.mult, op1=ALU.mult))
        then(nc.vector.scalar_tensor_tensor(out=out, in0=t, scalar=1.5, in1=out, op0=ALU.add, op1=ALU.mult))


def ln_statistics(nc, st, m, stage):
    return {"part": m.sb(f"{stage}_ln_part", [S, 4, B]), "steps": m.sem(f"{stage}_ln_steps"), "st": st}


def ln_on_dve(nc, dve, ln):
    st = ln["st"]
    s6, part = st["stats"], ln["part"]
    nc.vector.tensor_tensor(part[:, 0, :], s6[:, :, 1], s6[:, :, 4], ALU.add)
    nc.vector.tensor_tensor(part[:, 1, :], s6[:, :, 1], s6[:, :, 4], ALU.subtract)
    nc.vector.tensor_tensor(part[:, 2, :], s6[:, :, 2], s6[:, :, 5], ALU.add).then_inc(ln["steps"], 1)
    dve.wait_ge(ln["steps"], 1)
    nc.vector.tensor_scalar(st["mean"][:], part[:, 0, :], 0.5, None, ALU.mult)
    nc.vector.tensor_tensor(part[:, 3, :], part[:, 1, :], part[:, 1, :], ALU.mult)
    nc.vector.tensor_scalar(part[:, 2, :], part[:, 2, :], 1.0 / D, EPS, ALU.mult, ALU.add).then_inc(ln["steps"], 1)
    dve.wait_ge(ln["steps"], 2)
    nc.vector.scalar_tensor_tensor(out=part[:, 1, :], in0=part[:, 3, :], scalar=0.25, in1=part[:, 2, :],
                                   op0=ALU.mult, op1=ALU.add).then_inc(ln["steps"], 1)
    dve.wait_ge(ln["steps"], 3)
    inverse_root(nc, dve, st["rstd"][:], part[:, 1, :], part[:, 2, :], ln["steps"], 3)


def normalise(nc, out, st, b0, count):
    for j in range(count):
        last = nc.vector.tensor_scalar(out[:, j, :], st["h"][:, ds(b0 + j, 1), :].rearrange("p a b -> p (a b)"),
                                       st["mean"][:, ds(b0 + j, 1)], st["rstd"][:, ds(b0 + j, 1)], ALU.subtract, ALU.mult)
    return last


def token_statistics(nc, st, b0, count):
    for j in range(count):
        last = nc.vector.bn_stats(st["stats"][:, ds(b0 + j, 1), :].rearrange("p a b -> p (a b)"),
                                  st["h"][:, ds(b0 + j, 1), :].rearrange("p a b -> p (a b)"))
    return last


def attention(nc, io, st):
    h, ident = st["h"], st["ident"]
    with ExitStack() as ctx:
        m = Mem(nc, ctx)
        wq, wk, wv = m.sb("wq", [D, D]), m.sb("wk", [D, D]), m.sb("wv", [D, D])
        bq, bk, bv = m.sb("bq", [D, 1]), m.sb("bk", [D, 1]), m.sb("bv", [S, D])
        sinus = m.sb("sinus", [D, S])
        xn = [m.sb(f"a_xn{i}", [S, G, D]) for i in range(2)]
        xt = [m.sb(f"a_xt{i}", [D, W]) for i in range(2)]
        qt = [m.sb(f"a_qt{i}", [D, W]) for i in range(2)]
        kt = [m.sb(f"a_kt{i}", [D, W]) for i in range(2)]
        v = [m.sb(f"a_v{i}", [S, G, D]) for i in range(2)]
        neg = [m.sb(f"a_neg{i}", [S, G]) for i in range(2)]
        tot = [m.sb(f"a_tot{i}", [S, G]) for i in range(2)]
        inv = [m.sb(f"a_inv{i}", [S, G]) for i in range(2)]
        ex = [m.sb(f"a_ex{i}", [S, G, S]) for i in range(2)]
        pr = [m.sb(f"a_pr{i}", [S, G, S]) for i in range(2)]
        pt = [m.sb(f"a_pt{i}", [S, G, S]) for i in range(2)]
        p_x, p_q, p_k = m.ps("a_px", [D, W]), m.ps("a_pq", [D, W]), m.ps("a_pk", [D, W])
        p_v, p_s = m.ps("a_pv", [S, G, D]), m.ps("a_ps", [S, G, S])
        p_t, p_o = m.ps("a_ppt", [S, G, S]), m.ps("a_po", [S, G, D])
        ln = ln_statistics(nc, st, m, "a")
        w_in = m.sem("a_weights_in")
        normed, x_turned, x_ready = m.sem("a_normed"), m.sem("a_x_turned"), m.sem("a_x_ready")
        projected, qk_ready, v_ready = m.sem("a_projected"), m.sem("a_qk_ready"), m.sem("a_v_ready")
        scored, maxed, exped, inverted = m.sem("a_scored"), m.sem("a_maxed"), m.sem("a_exped"), m.sem("a_inverted")
        probs_ready, probs_turned, pt_ready = m.sem("a_probs_ready"), m.sem("a_probs_turned"), m.sem("a_pt_ready")
        mixed, added, stats_made = m.sem("a_mixed"), m.sem("a_added"), m.sem("a_stats_made")
        with nc.Block() as block:

            @block.sync
            def _(sp):
                for t, src in ((wq, io["wq_t"]), (wk, io["wk_t"]), (wv, io["wv_t"]), (bq, io["bq"].unsqueeze(1)), (bk, io["bk"].unsqueeze(1)),
                               (bv, row_broadcast(io["bv"], S)), (sinus, io["sinus_t"])):
                    sp.dma_start(t[:], src).then_inc(w_in, 16)

            @block.vector
            def _(dve):
                ln_on_dve(nc, dve, ln)
                dve.wait_ge(w_in, 7 * 16)

                def norm(g, p, j2):
                    wait(dve, x_turned, g - 1)
                    normalise(nc, xn[p], st, g * G, G).then_inc(normed, 1)

                def place(g, p, j2):
                    dve.wait_ge(x_turned, g + 1)
                    wait(dve, projected, g - 1)
                    nc.vector.tensor_tensor(xt[p][:].rearrange("p (a b) -> p a b", a=G), p_x[:].rearrange("p (a b) -> p a b", a=G),
                                            bc(sinus[:], 1, G), ALU.add).then_inc(x_ready, 1)

                def v_bias(g, p, j2):
                    dve.wait_ge(projected, g + 1)
                    wait(dve, mixed, g - 1)
                    nc.vector.tensor_tensor(v[p][:], p_v[:], bc(bv[:], 1, G), ALU.add).then_inc(v_ready, 1)

                def row_max(g, p, j2):
                    dve.wait_ge(scored, g + 1)
                    wait(dve, exped, g - 1)
                    nc.vector.tensor_reduce(neg[p][:], p_s[:], X, ALU.max, negate=True).then_inc(maxed, 1)

                def invert(g, p, j2):
                    dve.wait_ge(exped, g + 1)
                    wait(dve, probs_ready, g - 1)
                    nc.vector.reciprocal(inv[p][:], tot[p][:]).then_inc(inverted, 1)

                def add(g, p, j2):
                    dve.wait_ge(mixed, g + 1)
                    nc.vector.tensor_tensor(h[:, ds(g * G, G), :], h[:, ds(g * G, G), :], p_o[:], ALU.add).then_inc(added, 1)

                def statistics(g, p, j2):
                    dve.wait_ge(added, g + 1)
                    token_statistics(nc, st, g * G, G).then_inc(stats_made, 1)

                ticks(dve, NG, [(3, row_max), (4, add), (0, norm), (3, invert), (4, statistics), (2, v_bias), (1, place)])

            @block.gpsimd
            def _(pool):
                def divide(g, p, j2):
                    pool.wait_ge(inverted, g + 1)
                    wait(pool, probs_turned, g - 1)
                    nc.gpsimd.tensor_tensor(pr[p][:], ex[p][:], bc(inv[p][:], 2, S), ALU.mult).then_inc(probs_ready, 1)

                ticks(pool, NG, [(0, divide)])

            @block.scalar
            def _(act):
                act.wait_ge(w_in, 7 * 16)

                def qk_bias(g, p, j2):
                    act.wait_ge(projected, g + 1)
                    wait(act, scored, g - 1)
                    nc.scalar.activation(qt[p][:], p_q[:], ACT.Identity, bias=bq[:, 0:1])
                    nc.scalar.activation(kt[p][:], p_k[:], ACT.Identity, bias=bk[:, 0:1]).then_inc(qk_ready, 1)

                def exponent(g, p, j2):
                    act.wait_ge(maxed, g + 1)
                    wait(act, probs_ready, g - 1)
                    for j in range(G):
                        last = nc.scalar.activation(ex[p][:, j, :], p_s[:, j, :], ACT.Exp, bias=neg[p][:, j:j + 1], accum_out=tot[p][:, j:j + 1])
                    last.then_inc(exped, 1)

                def keep_pt(g, p, j2):
                    act.wait_ge(probs_turned, g + 1)
                    wait(act, mixed, g - 1)
                    nc.scalar.copy(pt[p][:], p_t[:]).then_inc(pt_ready, 1)

                ticks(act, NG, [(1, exponent), (0, qk_bias), (1, keep_pt)])

            @block.tensor
            def _(pe):
                pe.wait_ge(w_in, 7 * 16)

                def turn_x(g, p, j2):
                    pe.wait_ge(normed, g + 1)
                    wait(pe, x_ready, g)
                    for j in range(G):
                        last = nc.tensor.transpose(p_x[:, j * S:(j + 1) * S], xn[p][:, j, :], ident[0:S, 0:S])
                    last.then_inc(x_turned, 1)

                def project(g, p, j2):
                    pe.wait_ge(x_ready, g + 1)
                    wait(pe, qk_ready, g)
                    wait(pe, v_ready, g)
                    nc.tensor.matmul(p_q[:], wq[:], xt[p][:], start=True, stop=True)
                    nc.tensor.matmul(p_k[:], wk[:], xt[p][:], start=True, stop=True)
                    for j in range(G):
                        last = nc.tensor.matmul(p_v[:, j, :], xt[p][:, j * S:(j + 1) * S], wv[:], start=True, stop=True)
                    last.then_inc(projected, 1)

                def score(g, p, j2):
                    pe.wait_ge(qk_ready, g + 1)
                    wait(pe, exped, g)
                    for j in range(G):
                        c = slice(j * S, (j + 1) * S)
                        last = nc.tensor.matmul(p_s[:, j, :], qt[p][:, c], kt[p][:, c], start=True, stop=True)
                    last.then_inc(scored, 1)

                def turn_probs(g, p, j2):
                    pe.wait_ge(probs_ready, g + 1)
                    wait(pe, pt_ready, g)
                    for j in range(G):
                        last = nc.tensor.transpose(p_t[:, j, :], pr[p][:, j, :], ident[0:S, 0:S])
                    last.then_inc(probs_turned, 1)

                def mix(g, p, j2):
                    pe.wait_ge(pt_ready, g + 1)
                    pe.wait_ge(v_ready, g + 1)
                    wait(pe, added, g)
                    for j in range(G):
                        last = nc.tensor.matmul(p_o[:, j, :], pt[p][:, j, :], v[p][:, j, :], start=True, stop=True)
                    last.then_inc(mixed, 1)

                ticks(pe, NG, [(1, project), (2, turn_probs), (0, turn_x), (1, score), (2, mix)])

def route_to_experts(nc, io, st):
    ident, xg, selt = st["ident"], st["xg"], st["selt"]
    with ExitStack() as ctx:
        m = Mem(nc, ctx)
        gate, iota = m.sb("r_gate", [D, E0]), m.sb("r_iota", [128, S])
        identb = m.sb("r_identb", [128, 128], BF16)
        xn = [m.sb(f"r_xn{i}", [S, TI, D]) for i in range(2)]
        xt = m.sb("r_xt", [D, TI * S])
        neg, tot, inv = m.sb("r_neg", [S, TI]), m.sb("r_tot", [S, TI]), m.sb("r_inv", [S, TI])
        lg, ex, aff = m.sb("r_lg", [S, TI, E0]), m.sb("r_ex", [S, TI, E0]), [m.sb(f"r_aff{i}", [S, TI, E0]) for i in range(2)]
        aft, top = m.sb("r_aft", [128, S]), m.sb("r_top", [128, K0])
        idx, idxf = m.sb("r_idx", [128, K0], U32), m.sb("r_idxf", [128, K0])
        spare = m.sb("r_spare", [128, 1])
        oh = m.sb("r_onehot", [128, K0, S], BF16)
        sel, selw = m.sb("r_sel", [S, TI, K0 * E0]), m.sb("r_selw", [S, TI, K0 * E0])
        p_x = [m.ps(f"r_px{i}", [D, W]) for i in range(2)]
        p_small = m.ps("r_psmall", [128, 512])
        p_l, p_a = p_small[0:S, 0:TI * E0].rearrange("p (a b) -> p a b", a=TI), p_small[:, 256:256 + S]
        p_sel = m.ps("r_psel", [S, K0, 128], BF16)
        p_g = [m.ps(f"r_pg{i}", [D, G, K0, E0]) for i in range(2)]
        p_w = [m.ps(f"r_pw{i}", [128, G, S]) for i in range(2)]
        ln = ln_statistics(nc, st, m, "r")
        w_in, cast = m.sem("r_weights_in"), m.sem("r_identb_made")
        normed, x_turned, x_ready = m.sem("r_normed"), m.sem("r_x_turned"), m.sem("r_x_ready")
        gated, maxed, shifted, exped = m.sem("r_gated"), m.sem("r_maxed"), m.sem("r_shifted"), m.sem("r_exped")
        summed, inverted, aff_ready = m.sem("r_summed"), m.sem("r_inverted"), m.sem("r_aff_ready")
        aff_turned, aft_ready, topped = m.sem("r_aff_turned"), m.sem("r_aft_ready"), m.sem("r_topped")
        indexed, idxf_ready, oh_ready = m.sem("r_indexed"), m.sem("r_idxf_ready"), m.sem("r_onehot_ready")
        oh_turned, sel_ready, selw_ready = m.sem("r_onehot_turned"), m.sem("r_sel_ready"), m.sem("r_selw_ready")
        gathered, xg_kept, selw_turned, selt_kept = m.sem("r_gathered"), m.sem("r_xg_kept"), m.sem("r_selw_turned"), m.sem("r_selt_kept")
        NT = B // TI
        with nc.Block() as block:

            @block.sync
            def _(sp):
                sp.dma_start(gate[:], io["gate"]).then_inc(w_in, 16)
                sp.dma_start(iota[:], row_broadcast(io["iota"], 128)).then_inc(w_in, 16)

            @block.vector
            def _(dve):
                nc.vector.tensor_copy(identb[:], ident[:]).then_inc(cast, 1)
                ln_on_dve(nc, dve, ln)
                dve.wait_ge(w_in, 32)

                def norm(g, p, j2):
                    wait(dve, gathered, g - 1)
                    normalise(nc, xn[p], st, g * TI, TI).then_inc(normed, 1)

                def softmax(g, p, j2):
                    dve.wait_ge(gated, g + 1)
                    nc.vector.tensor_reduce(neg[:], p_l, X, ALU.max, negate=True).then_inc(maxed, 1)
                    dve.wait_ge(maxed, g + 1)
                    wait(dve, exped, g)
                    nc.vector.tensor_tensor(lg[:], p_l, bc(neg[:], 2, E0), ALU.add).then_inc(shifted, 1)

                def divide(g, p, j2):
                    dve.wait_ge(exped, g + 1)
                    nc.vector.tensor_reduce(tot[:], ex[:], X, ALU.add).then_inc(summed, 1)
                    dve.wait_ge(summed, g + 1)
                    nc.vector.reciprocal(inv[:], tot[:]).then_inc(inverted, 1)
                    dve.wait_ge(inverted, g + 1)
                    wait(dve, aff_turned, g - 1)
                    nc.vector.tensor_tensor(aff[p][:], ex[:], bc(inv[:], 2, E0), ALU.mult).then_inc(aff_ready, 1)

                def choose(g, p, j2):
                    dve.wait_ge(aff_turned, g + 1)
                    nc.vector.tensor_copy(aft[:], p_a).then_inc(aft_ready, 1)
                    dve.wait_ge(aft_ready, g + 1)
                    nc.vector.memset(spare[:], 0.0)
                    nc.vector.max(top[:], aft[:]).then_inc(topped, 1)
                    dve.wait_ge(topped, g + 1)
                    nc.vector.memset(spare[:], 0.0)
                    nc.vector.max_index(idx[:], top[:], aft[:]).then_inc(indexed, 1)
                    dve.wait_ge(indexed, g + 1)
                    nc.vector.tensor_copy(idxf[:], idx[:]).then_inc(idxf_ready, 1)
                    dve.wait_ge(idxf_ready, g + 1)
                    wait(dve, oh_turned, g)
                    nc.vector.tensor_tensor(oh[:], bc(iota[:], 1, K0), bc(idxf[:], 2, S), ALU.is_equal).then_inc(oh_ready, 1)

                def weigh(g, p, j2):
                    dve.wait_ge(sel_ready, g + 1)
                    wait(dve, selw_turned, g)
                    nc.vector.tensor_tensor(selw[:].rearrange("p a (k e) -> p a k e", k=K0), sel[:].rearrange("p a (k e) -> p a k e", k=K0),
                                            bc(aff[p][:], 2, K0), ALU.mult).then_inc(selw_ready, 1)

                def keep_selt(g, p, j2):
                    dve.wait_ge(selw_turned, g + 1)
                    for i in range(2):
                        last = nc.vector.tensor_copy(selt[:, ds(g * TI + i * G, G), :], p_w[i][:])
                    last.then_inc(selt_kept, 1)

                ticks(dve, NT, [(1, softmax), (2, weigh), (1, divide), (3, keep_selt), (1, choose), (0, norm)])

            @block.scalar
            def _(act):
                def keep_x(g, p, j2):
                    act.wait_ge(x_turned, g + 1)
                    wait(act, gated, g)
                    for i in range(2):
                        last = nc.scalar.copy(xt[:, i * W:(i + 1) * W], p_x[i][:])
                    last.then_inc(x_ready, 1)

                def exponent(g, p, j2):
                    act.wait_ge(shifted, g + 1)
                    wait(act, aff_ready, g)
                    nc.scalar.activation(ex[:], lg[:], ACT.Exp).then_inc(exped, 1)

                def keep_sel(g, p, j2):
                    act.wait_ge(oh_turned, g + 1)
                    wait(act, selw_ready, g)
                    wait(act, gathered, g)
                    nc.scalar.copy(sel[:].rearrange("p a (k e) -> p k a e", k=K0), p_sel[:].rearrange("p k (a e) -> p k a e", a=TI)).then_inc(sel_ready, 1)

                def keep_g(g, p, j2):
                    act.wait_ge(gathered, g + 1)
                    for i in range(2):
                        last = nc.scalar.copy(xg[:, :, ds(g * TI + i * G, G), :], p_g[i][:].rearrange("p a k e -> p e a k"))
                    last.then_inc(xg_kept, 1)

                ticks(act, NT, [(1, exponent), (2, keep_g), (1, keep_sel), (0, keep_x)])

            @block.tensor
            def _(pe):
                pe.wait_ge(w_in, 32)
                pe.wait_ge(cast, 1)

                def turn_x(g, p, j2):
                    pe.wait_ge(normed, g + 1)
                    wait(pe, x_ready, g)
                    for j in range(TI):
                        last = nc.tensor.transpose(p_x[j // G][:, j % G * S:(j % G + 1) * S], xn[p][:, j, :], ident[0:S, 0:S])
                    last.then_inc(x_turned, 1)

                def gates(g, p, j2):
                    pe.wait_ge(x_ready, g + 1)
                    wait(pe, shifted, g)
                    wait(pe, aft_ready, g)
                    for j in range(TI):
                        last = nc.tensor.matmul(p_l[:, j, :], xt[:, j * S:(j + 1) * S], gate[:], start=True, stop=True)
                    last.then_inc(gated, 1)

                def turn_aff(g, p, j2):
                    pe.wait_ge(aff_ready, g + 1)
                    nc.tensor.transpose(p_a, aff[p][:].rearrange("p a b -> p (a b)"), ident[0:S, 0:S]).then_inc(aff_turned, 1)

                def turn_onehot(g, p, j2):
                    pe.wait_ge(oh_ready, g + 1)
                    wait(pe, sel_ready, g)
                    for k in range(K0):
                        last = nc.tensor.transpose(p_sel[:, k, :], oh[:, k, :], identb[:])
                    last.then_inc(oh_turned, 1)

                def gather(half):
                    def step(g, p, j2):
                        pe.wait_ge(sel_ready, g + 1)
                        wait(pe, xg_kept, g)
                        for j in range(G):
                            last = nc.tensor.matmul(p_g[half][:, j].rearrange("p k e -> p (k e)"), xn[p][:, half * G + j, :], sel[:, half * G + j, :],
                                                    start=True, stop=True)
                        if half == 1:
                            last.then_inc(gathered, 1)
                    return step

                def turn_selw(g, p, j2):
                    pe.wait_ge(selw_ready, g + 1)
                    wait(pe, selt_kept, g)
                    for j in range(TI):
                        last = nc.tensor.transpose(p_w[j // G][:, j % G, :], selw[:, j, :], ident[0:S, 0:S])
                    last.then_inc(selw_turned, 1)

                ticks(pe, NT, [(1, gates), (2, gather(0)), (1, turn_aff), (2, gather(1)), (2, turn_selw), (1, turn_onehot), (0, turn_x)])


def expert_layers(nc, io, st):
    xg = st["xg"]
    N = B * K0 // 2
    with ExitStack() as ctx:
        m = Mem(nc, ctx)
        w1 = [m.sb(f"e_w1_{i}", [D, D]) for i in range(2)]
        w2 = [m.sb(f"e_w2_{i}", [D, D]) for i in range(2)]
        b1, b2 = m.sb("e_b1", [D, E0]), m.sb("e_b2", [D, E0])
        ht = [m.sb(f"e_h{i}", [D, 2, N]) for i in range(2)]
        p_h = [[m.ps(f"e_ph{i}{j}", [D, N]) for j in range(2)] for i in range(2)]
        p_y = [[m.ps(f"e_py{i}{j}", [D, N]) for j in range(2)] for i in range(2)]
        b_in, w_in = m.sem("e_bias_in"), [m.sem(f"e_weights_in{i}") for i in range(2)]
        up_done, h_ready, down_done, y_kept = m.sem("e_up"), m.sem("e_h_ready"), m.sem("e_down"), m.sem("e_y_kept")
        flat = xg[:].rearrange("p e b k -> p e (b k)")
        with nc.Block() as block:

            @block.sync
            def _(sp):
                sp.dma_start(b1[:], io["b1_t"]).then_inc(b_in, 16)
                sp.dma_start(b2[:], io["b2_t"]).then_inc(b_in, 16)

                def load(g, p, j2):
                    wait(sp, down_done, g - 1)
                    for t, src in ((w1, io["w1"]), (w2, io["w2"])):
                        sp.dma_start(t[p][:], src[ds(g, 1)].squeeze(0)).then_inc(w_in[p], 16)

                ticks(sp, E0, [(0, load)])

            @block.tensor
            def _(pe):
                def up(g, p, j2):
                    pe.wait_ge(w_in[p], j2 * 32 + 32)
                    wait(pe, h_ready, g - 1)
                    for i in range(2):
                        last = nc.tensor.matmul(p_h[p][i][:], w1[p][:], flat[:, ds(g, 1), i * N:(i + 1) * N].rearrange("p a b -> p (a b)"), start=True, stop=True)
                    last.then_inc(up_done, 1)

                def down(g, p, j2):
                    pe.wait_ge(h_ready, g + 1)
                    wait(pe, y_kept, g - 1)
                    for i in range(2):
                        last = nc.tensor.matmul(p_y[p][i][:], w2[p][:], ht[p][:, i, :], start=True, stop=True)
                    last.then_inc(down_done, 1)

                ticks(pe, E0, [(0, up), (1, down)])

            @block.scalar
            def _(act):
                act.wait_ge(b_in, 32)

                def gelu(g, p, j2):
                    act.wait_ge(up_done, g + 1)
                    wait(act, down_done, g - 1)
                    for i in range(2):
                        last = nc.scalar.activation(ht[p][:, i, :], p_h[p][i][:], ACT.Gelu_apprx_tanh, bias=b1[:, ds(g, 1)])
                    last.then_inc(h_ready, 1)

                ticks(act, E0, [(0, gelu)])

            @block.vector
            def _(dve):
                dve.wait_ge(b_in, 32)

                def keep(g, p, j2):
                    dve.wait_ge(down_done, g + 1)
                    for i in range(2):
                        last = nc.vector.tensor_scalar(flat[:, ds(g, 1), i * N:(i + 1) * N].rearrange("p a b -> p (a b)"), p_y[p][i][:], b2[:, ds(g, 1)], None, ALU.add)
                    last.then_inc(y_kept, 1)

                ticks(dve, E0, [(0, keep)])


def gather_experts(nc, io, st):
    h, ident, xg, selt = st["h"], st["ident"], st["xg"], st["selt"]
    with ExitStack() as ctx:
        m = Mem(nc, ctx)
        xs = [m.sb(f"g_xs{i}", [D, TI, K0 * E0]) for i in range(2)]
        ss = [m.sb(f"g_ss{i}", [128, TI, S]) for i in range(2)]
        ys = m.sb("g_ys", [128, TI, D])
        p_y = [m.ps(f"g_py{i}", [128, G, D]) for i in range(2)]
        p_o = [m.ps(f"g_po{i}", [S, G, D]) for i in range(2)]
        xs_ready, ss_ready, y_turned, y_kept = m.sem("g_xs_ready"), m.sem("g_ss_ready"), m.sem("g_y_turned"), m.sem("g_y_kept")
        scattered, added, stats_made = m.sem("g_scattered"), m.sem("g_added"), m.sem("g_stats_made")
        NT = B // TI
        with nc.Block() as block:

            @block.scalar
            def _(act):
                def arrange(g, p, j2):
                    wait(act, y_turned, g - 1)
                    nc.scalar.copy(xs[p][:].rearrange("p a (k e) -> p a k e", k=K0),
                                   xg[:, :, ds(g * TI, TI), :].rearrange("p e a k -> p a k e")).then_inc(xs_ready, 1)

                def keep_y(g, p, j2):
                    act.wait_ge(y_turned, g + 1)
                    wait(act, scattered, g)
                    for i in range(2):
                        last = nc.scalar.copy(ys[:, i * G:(i + 1) * G, :], p_y[i][:])
                    last.then_inc(y_kept, 1)

                ticks(act, NT, [(0, arrange), (1, keep_y)])

            @block.vector
            def _(dve):
                def stage(g, p, j2):
                    wait(dve, scattered, g - 1)
                    nc.vector.tensor_copy(ss[p][:], selt[:, ds(g * TI, TI), :]).then_inc(ss_ready, 1)

                def add(g, p, j2):
                    dve.wait_ge(scattered, g + 1)
                    for i in range(2):
                        hs = h[:, ds(g * TI + i * G, G), :]
                        last = nc.vector.tensor_tensor(hs, hs, p_o[i][:], ALU.add)
                    last.then_inc(added, 1)
                    dve.wait_ge(added, g + 1)
                    token_statistics(nc, st, g * TI, TI).then_inc(stats_made, 1)

                ticks(dve, NT, [(0, stage), (1, add)])

            @block.tensor
            def _(pe):
                def turn_y(g, p, j2):
                    pe.wait_ge(xs_ready, g + 1)
                    wait(pe, y_kept, g)
                    for j in range(TI):
                        last = nc.tensor.transpose(p_y[j // G][:, j % G, :], xs[p][:, j, :], ident[:])
                    last.then_inc(y_turned, 1)

                def scatter(g, p, j2):
                    pe.wait_ge(y_kept, g + 1)
                    pe.wait_ge(ss_ready, g + 1)
                    wait(pe, added, g)
                    for j in range(TI):
                        last = nc.tensor.matmul(p_o[j // G][:, j % G, :], ss[p][:, j, :], ys[:, j, :], start=True, stop=True)
                    last.then_inc(scattered, 1)

                ticks(pe, NT, [(0, turn_y), (0, scatter)])


def expert_choice(nc, io, st):
    with ExitStack() as ctx:
        m = Mem(nc, ctx)
        st = dict(st, xg=m.sb("xg", [D, E0, B, K0]), selt=m.sb("selt", [128, B, S]))
        route_to_experts(nc, io, st)
        expert_layers(nc, io, st)
        gather_experts(nc, io, st)

def upto(n, most):
    return min(n, most) if isinstance(n, int) else n


def retention(nc, io, st):
    h, ident = st["h"], st["ident"]
    with ExitStack() as ctx:
        m = Mem(nc, ctx)
        names = ("wq1", "wq1_turn", "wk1", "wk1_turn", "wv1", "wg1", "wo1")
        wt = {n: m.sb(n, [D, D]) for n in names}
        tabs = {n: m.sb(n, [D, S]) for n in ("cos_q", "sin_q", "cos_k", "sin_k")}
        decay = m.sb("decay", [S, 2, NH // 2, S])
        mask, gnw, gnb = m.sb("head_mask", [D, 2]), m.sb("gnw", [D, 1]), m.sb("gnb", [D, 1])
        xn = [m.sb(f"t_xn{i}", [S, G, D]) for i in range(2)]
        xt = [m.sb(f"t_xt{i}", [D, W]) for i in range(2)]
        qc, qs, kc, ks, kt = (m.sb(f"t_{n}", [D, W]) for n in ("qc", "qs", "kc", "ks", "kt"))
        qt = [m.sb(f"t_qt{i}", [D, W]) for i in range(2)]
        km = [m.sb(f"t_km{i}", [D, G, NH, S]) for i in range(2)]
        v_pair = [m.sb(f"t_vpair{i}", [2 * NP, G, NH // 2, 2 * DH]) for i in range(2)]
        v_cls = [m.sb(f"t_vcls{i}", [NH, G, D]) for i in range(2)]
        own = m.sb("t_own", [NH, D])
        th = m.sb("t_th", [D, W])
        swish = m.sb("t_swish", [D, NG, W])
        neg = [m.sb(f"t_neg{i}", [S, 2, NH // 2]) for i in range(2)]
        lg = [m.sb(f"t_lg{i}", [S, 2, NH // 2, S]) for i in range(2)]
        pt = [m.sb(f"t_pt{i}", [2 * NP, NH // 2, S]) for i in range(2)]
        pt_cls = [m.sb(f"t_ptcls{i}", [NH, S]) for i in range(2)]
        ex = [m.sb(f"t_ex{i}", [S, 2, NH // 2, S]) for i in range(G)]
        pd, pd_cls = [m.sb(f"t_pd{i}", [S, NH, NP]) for i in range(G)], [m.sb(f"t_pdcls{i}", [S, NH]) for i in range(G)]
        tot = [m.sb(f"t_tot{i}", [S, G, NH]) for i in range(2)]
        inv, mu, ss, ve, rs = (m.sb(f"t_{n}", [S, G * NH]) for n in ("inv", "mu", "ss", "ve", "rs"))
        y, yc, sq, yh = (m.sb(f"t_{n}", [S, G * NH, DH]) for n in ("y", "yc", "sq", "yh"))
        u1, u = m.sb("t_u1", [D, W]), m.sb("t_u", [D, W])
        pm0, pm1, pm2, p_y = (m.ps(n, [128, 512]) for n in ("t_pm0", "t_pm1", "t_pm2", "t_py"))
        p_s, p_t, p_vc = m.ps("t_ps", [S, 2, 512]), m.ps("t_pt", [2 * NP, NH // 2 + 1, S]), m.ps("t_pvc", [NH, G, D])
        scores = p_s[:, :, 0:W].rearrange("p a (b c) -> p a b c", c=S)
        ln = ln_statistics(nc, st, m, "t")
        sems = ("weights_in", "zeroed", "normed", "x_turned", "x_ready", "q_made", "q_read", "q_ready", "k_made", "k_read", "kt_ready",
                "km_ready", "v_made", "v_ready", "v_cls_ready", "g_made", "tanh_ready", "swish_ready", "scored", "maxed",
                "shifted", "exped", "summed", "decayed", "p_turned", "pt_kept", "mixed", "inv_ready", "y_ready", "mu_ready",
                "yc_ready", "sq_ready", "ss_ready", "ve_ready", "rs_ready", "yh_ready", "y_turned", "u1_ready", "u_ready", "out_made",
                "added", "stats_made")
        s = {n: m.sem("t_" + n) for n in sems}
        n_in = 16 * (len(names) + 4 + 5)

        def images(t, a=G):
            return t.rearrange("p (a b) -> p a b", a=a)

        with nc.Block() as block:

            @block.sync
            def _(sp):
                for n in names:
                    sp.dma_start(wt[n][:], io[n]).then_inc(s["weights_in"], 16)
                for n in tabs:
                    sp.dma_start(tabs[n][:], io[n]).then_inc(s["weights_in"], 16)
                sp.dma_start(decay[:], io["decay"]).then_inc(s["weights_in"], 16)
                sp.dma_start(mask[:], io["head_mask"]).then_inc(s["weights_in"], 16)
                sp.dma_start(own[:], io["own_channels"]).then_inc(s["weights_in"], 16)
                sp.dma_start(gnw[:], io["gnw"].unsqueeze(1)).then_inc(s["weights_in"], 16)
                sp.dma_start(gnb[:], io["gnb"].unsqueeze(1)).then_inc(s["weights_in"], 16)

            @block.vector
            def _(dve):
                ln_on_dve(nc, dve, ln)
                dve.wait_ge(s["weights_in"], n_in)

                def norm(g, p, j2):
                    wait(dve, s["x_turned"], g - 1)
                    normalise(nc, xn[p], st, g * G, G).then_inc(s["normed"], 1)

                def rotate_q(g, p, j2):
                    dve.wait_ge(s["q_made"], g + 1)
                    wait(dve, s["q_ready"], g)
                    nc.vector.tensor_tensor(images(qc[:]), images(pm1[:, 0:W]), bc(tabs["cos_q"][:], 1, G), ALU.mult)
                    nc.vector.tensor_tensor(images(qs[:]), images(pm2[:, 0:W]), bc(tabs["sin_q"][:], 1, G), ALU.mult).then_inc(s["q_read"], 1)

                def rotate_k(g, p, j2):
                    dve.wait_ge(s["k_made"], g + 1)
                    wait(dve, s["kt_ready"], g)
                    nc.vector.tensor_tensor(images(kc[:]), images(pm1[:, 0:W]), bc(tabs["cos_k"][:], 1, G), ALU.mult)
                    nc.vector.tensor_tensor(images(ks[:]), images(pm2[:, 0:W]), bc(tabs["sin_k"][:], 1, G), ALU.mult).then_inc(s["k_read"], 1)

                def gate(g, p, j2):
                    dve.wait_ge(s["tanh_ready"], g + 1)
                    nc.vector.scalar_tensor_tensor(out=swish[:, ds(g, 1), :].rearrange("p a b -> p (a b)"), in0=th[:], scalar=1.0, in1=pm2[:, 0:W],
                                                   op0=ALU.add, op1=ALU.mult).then_inc(s["swish_ready"], 1)

                def keep_v_cls(g, p, j2):
                    dve.wait_ge(s["v_made"], g + 1)
                    wait(dve, s["mixed"], (g - 1) * G)
                    nc.vector.tensor_tensor(v_cls[p][:], p_vc[:], bc(own[:], 1, G), ALU.mult).then_inc(s["v_cls_ready"], 1)

                def shift(j):
                    def step(g, p, j2):
                        n, q = g * G + j, j % 2
                        dve.wait_ge(s["scored"], n + 1)
                        nc.vector.tensor_reduce(neg[q][:], scores, X, ALU.max, negate=True).then_inc(s["maxed"], 1)
                        dve.wait_ge(s["maxed"], n + 1)
                        wait(dve, s["exped"], n - 1)
                        nc.vector.tensor_tensor(lg[q][:], scores, bc(neg[q][:], 3, S), ALU.add).then_inc(s["shifted"], 1)
                    return step

                def total(j):
                    def step(g, p, j2):
                        n = g * G + j
                        dve.wait_ge(s["exped"], n + 1)
                        if j == 0:
                            wait(dve, s["inv_ready"], g - 1)
                        nc.vector.tensor_reduce(tot[p][:, j, :].rearrange("p (a b) -> p a b", a=2), ex[j][:], X, ALU.add).then_inc(s["summed"], 1)
                    return step

                def divide(g, p, j2):
                    dve.wait_ge(s["summed"], g * G + G)
                    wait(dve, s["y_ready"], g)
                    nc.vector.reciprocal(inv[:], tot[p][:].rearrange("p a b -> p (a b)")).then_inc(s["inv_ready"], 1)
                    dve.wait_ge(s["inv_ready"], g + 1)
                    dve.wait_ge(s["mixed"], g * G + G)
                    nc.vector.tensor_tensor(y[:], p_y[0:S, :].rearrange("p (a b) -> p a b", b=DH), bc(inv[:], 2, DH), ALU.mult).then_inc(s["y_ready"], 1)

                def center(g, p, j2):
                    dve.wait_ge(s["y_ready"], g + 1)
                    nc.vector.tensor_reduce(mu[:], y[:], X, ALU.add).then_inc(s["mu_ready"], 1)
                    dve.wait_ge(s["mu_ready"], g + 1)
                    nc.vector.scalar_tensor_tensor(out=yc[:], in0=bc(mu[:], 2, DH), scalar=-1.0 / DH, in1=y[:], op0=ALU.mult,
                                                   op1=ALU.add).then_inc(s["yc_ready"], 1)

                def variance(g, p, j2):
                    dve.wait_ge(s["sq_ready"], g + 1)
                    nc.vector.tensor_reduce(ss[:], sq[:], X, ALU.add).then_inc(s["ss_ready"], 1)
                    dve.wait_ge(s["ss_ready"], g + 1)
                    nc.vector.tensor_scalar(ve[:], ss[:], 1.0 / DH, EPS, ALU.mult, ALU.add).then_inc(s["ve_ready"], 1)

                def head_norm(g, p, j2):
                    dve.wait_ge(s["rs_ready"], 2 * g + 2)
                    wait(dve, s["y_turned"], g)
                    nc.vector.tensor_tensor(yh[:], yc[:], bc(rs[:], 2, DH), ALU.mult).then_inc(s["yh_ready"], 1)

                def affine(g, p, j2):
                    dve.wait_ge(s["u1_ready"], g + 1)
                    wait(dve, s["out_made"], g)
                    nc.vector.scalar_tensor_tensor(out=u[:], in0=u1[:], scalar=0.5, in1=swish[:, ds(g, 1), :].rearrange("p a b -> p (a b)"),
                                                   op0=ALU.mult, op1=ALU.mult).then_inc(s["u_ready"], 1)

                def add(g, p, j2):
                    dve.wait_ge(s["out_made"], g + 1)
                    hs = h[:, ds(g * G, G), :]
                    nc.vector.tensor_tensor(hs, hs, pm0[0:S, :].rearrange("p (a b) -> p a b", a=G), ALU.add).then_inc(s["added"], 1)

                def statistics(g, p, j2):
                    dve.wait_ge(s["added"], g + 1)
                    token_statistics(nc, st, g * G, G).then_inc(s["stats_made"], 1)

                ticks(dve, NG, [
                    (3, shift(0)), (4, total(3)), (2, rotate_q), (5, center),
                    (3, shift(1)), (3, total(0)), (2, rotate_k), (5, variance), (7, statistics),
                    (3, shift(2)), (6, affine), (3, total(1)), (0, norm),
                    (3, shift(3)), (6, add), (2, keep_v_cls), (2, gate), (3, total(2)), (5, head_norm), (4, divide)])

            @block.gpsimd
            def _(pool):
                for p in range(2):
                    nc.gpsimd.memset(km[p][:], 0.0).then_inc(s["zeroed"], 1)
                    nc.gpsimd.memset(v_pair[p][:], 0.0).then_inc(s["zeroed"], 1)
                pool.wait_ge(s["weights_in"], n_in)

                def add_q(g, p, j2):
                    pool.wait_ge(s["q_read"], g + 1)
                    wait(pool, s["scored"], (g - 1) * G)
                    nc.gpsimd.tensor_tensor(qt[p][:], qc[:], qs[:], ALU.add).then_inc(s["q_ready"], 1)

                def add_k(g, p, j2):
                    pool.wait_ge(s["k_read"], g + 1)
                    wait(pool, s["km_ready"], 2 * g)
                    nc.gpsimd.tensor_tensor(kt[:], kc[:], ks[:], ALU.add).then_inc(s["kt_ready"], 1)

                def fade(j):
                    def step(g, p, j2):
                        n = g * G + j
                        pool.wait_ge(s["exped"], n + 1)
                        wait(pool, s["p_turned"], n - 3)
                        nc.gpsimd.tensor_tensor(pd[j][:].rearrange("p (a b) c -> p a b c", a=2), ex[j][:, :, :, 1:S], decay[:, :, :, 1:S], ALU.mult)
                        nc.gpsimd.tensor_tensor(pd_cls[j][:].rearrange("p (a b) -> p a b", a=2), ex[j][:, :, :, 0], decay[:, :, :, 0],
                                                ALU.mult).then_inc(s["decayed"], 1)
                    return step

                def power(part):
                    c = slice(part * G * NH // 2, (part + 1) * G * NH // 2)

                    def step(g, p, j2):
                        pool.wait_ge(s["ve_ready"], g + 1)
                        wait(pool, s["yh_ready"], g)
                        nc.gpsimd.tensor_tensor(rs[:, c], ve[:, c], st["minus_half"][:, c], ALU.pow).then_inc(s["rs_ready"], 1)
                    return step

                ticks(pool, NG, [(3, fade(3)), (1, add_q), (2, fade(0)), (1, add_k), (4, power(0)), (2, fade(1)), (4, power(1)), (2, fade(2))])

            @block.scalar
            def _(act):
                act.wait_ge(s["weights_in"], n_in)
                act.wait_ge(s["zeroed"], 4)

                def keep_x(g, p, j2):
                    act.wait_ge(s["x_turned"], g + 1)
                    wait(act, s["g_made"], g - 1)
                    nc.scalar.copy(xt[p][:], pm0[:, 0:W]).then_inc(s["x_ready"], 1)

                def mask_k(part):
                    def step(g, p, j2):
                        act.wait_ge(s["kt_ready"], g + 1)
                        wait(act, s["scored"], (g - 1) * G)
                        for q in (2 * part, 2 * part + 1):
                            rows = slice(32 * q, 32 * q + 32)
                            for i in range(2):
                                last = nc.scalar.activation(km[p][rows, :, 2 * q + i, :], images(kt[rows, :]), ACT.Copy, scale=mask[rows, i:i + 1])
                        last.then_inc(s["km_ready"], 1)
                    return step

                def keep_v(g, p, j2):
                    act.wait_ge(s["v_made"], g + 1)
                    wait(act, s["mixed"], (g - 1) * G)
                    for i in range(2):
                        rows, cols = slice(i * NP, (i + 1) * NP), slice(i * DH, (i + 1) * DH)
                        last = nc.scalar.copy(v_pair[p][rows, :, :, cols].rearrange("p a b c -> p (a b) c"),
                                              pm1[rows, :].rearrange("p (a b) -> p a b", b=2 * DH)[:, :, cols])
                    last.then_inc(s["v_ready"], 1)

                def gate_tanh(g, p, j2):
                    act.wait_ge(s["g_made"], g + 1)
                    wait(act, s["swish_ready"], g)
                    nc.scalar.activation(th[:], pm2[:, 0:W], ACT.Tanh, scale=0.5).then_inc(s["tanh_ready"], 1)

                def exponent(j):
                    def step(g, p, j2):
                        n, q = g * G + j, j % 2
                        act.wait_ge(s["shifted"], n + 1)
                        wait(act, s["summed"], n - 3)
                        wait(act, s["decayed"], n - 3)
                        nc.scalar.activation(ex[j][:], lg[q][:], ACT.Exp).then_inc(s["exped"], 1)
                    return step

                def keep_pt(j):
                    def step(g, p, j2):
                        n, q = g * G + j, j % 2
                        act.wait_ge(s["p_turned"], n + 1)
                        wait(act, s["mixed"], n - 1)
                        nc.scalar.copy(pt[q][:], p_t[:, 0:NH // 2, :])
                        nc.scalar.copy(pt_cls[q][:], p_t[0:NH, NH // 2, :]).then_inc(s["pt_kept"], 1)
                    return step

                def scale_y(g, p, j2):
                    act.wait_ge(s["y_turned"], g + 1)
                    wait(act, s["u_ready"], g)
                    nc.scalar.activation(u1[:], pm0[:, 0:W], ACT.Identity, scale=gnw[:, 0:1], bias=gnb[:, 0:1]).then_inc(s["u1_ready"], 1)

                def square(g, p, j2):
                    act.wait_ge(s["yc_ready"], g + 1)
                    wait(act, s["ss_ready"], g)
                    nc.scalar.activation(sq[:], yc[:], ACT.Square).then_inc(s["sq_ready"], 1)

                ticks(act, NG, [
                    (3, keep_pt(1)), (2, exponent(0)),
                    (3, keep_pt(2)), (2, exponent(1)), (4, square), (5, scale_y), (1, mask_k(0)),
                    (3, keep_pt(3)), (2, exponent(2)), (1, mask_k(1)), (1, keep_v), (1, gate_tanh),
                    (2, keep_pt(0)), (2, exponent(3)), (0, keep_x)])

            @block.tensor
            def _(pe):
                pe.wait_ge(s["weights_in"], n_in)

                def turn_x(g, p, j2):
                    pe.wait_ge(s["normed"], g + 1)
                    wait(pe, s["x_ready"], g)
                    wait(pe, s["added"], g - 4)
                    for j in range(G):
                        last = nc.tensor.transpose(pm0[:, j * S:(j + 1) * S], xn[p][:, j, :], ident[0:S, 0:S])
                    last.then_inc(s["x_turned"], 1)

                def make_q(g, p, j2):
                    pe.wait_ge(s["x_ready"], g + 1)
                    wait(pe, s["v_ready"], g)
                    wait(pe, s["swish_ready"], g)
                    nc.tensor.matmul(pm1[:, 0:W], wt["wq1"][:], xt[p][:], start=True, stop=True)
                    nc.tensor.matmul(pm2[:, 0:W], wt["wq1_turn"][:], xt[p][:], start=True, stop=True).then_inc(s["q_made"], 1)

                def make_k(g, p, j2):
                    pe.wait_ge(s["q_read"], g + 1)
                    nc.tensor.matmul(pm1[:, 0:W], wt["wk1"][:], xt[p][:], start=True, stop=True)
                    nc.tensor.matmul(pm2[:, 0:W], wt["wk1_turn"][:], xt[p][:], start=True, stop=True).then_inc(s["k_made"], 1)

                def make_v(g, p, j2):
                    pe.wait_ge(s["k_read"], g + 1)
                    wait(pe, s["v_cls_ready"], g)
                    for j in range(G):
                        for i in range(2):
                            nc.tensor.matmul(pm1[i * NP:(i + 1) * NP, j * D:(j + 1) * D], xt[p][:, j * S + 1:(j + 1) * S], wt["wv1"][:], start=True, stop=True)
                        last = nc.tensor.matmul(p_vc[:, j, :], bc(xt[p][:, j * S], 1, NH), wt["wv1"][:], start=True, stop=True)
                    last.then_inc(s["v_made"], 1)
                    nc.tensor.matmul(pm2[:, 0:W], wt["wg1"][:], xt[p][:], start=True, stop=True).then_inc(s["g_made"], 1)

                def score(j):
                    def step(g, p, j2):
                        n = g * G + j
                        if j == 0:
                            pe.wait_ge(s["q_ready"], g + 1)
                            pe.wait_ge(s["km_ready"], 2 * g + 2)
                        wait(pe, s["shifted"], n)
                        for i in range(2):
                            last = nc.tensor.matmul(p_s[:, i, 0:W], qt[p][:, j * S:(j + 1) * S],
                                                    km[p][:, j, i * 4:i * 4 + 4, :].rearrange("p a b -> p (a b)"), start=True, stop=True)
                        last.then_inc(s["scored"], 1)
                    return step

                def turn_p(j):
                    def step(g, p, j2):
                        n = g * G + j
                        pe.wait_ge(s["decayed"], n + 1)
                        wait(pe, s["pt_kept"], n)
                        for i in range(NH // 2):
                            nc.tensor.transpose(p_t[:, i, :], pd[j][:, 2 * i:2 * i + 2, :].rearrange("p a b -> p (a b)"), ident[0:S, 0:S])
                        last = nc.tensor.transpose(p_t[0:NH, NH // 2, :], pd_cls[j][:], ident[0:S, 0:S])
                        last.then_inc(s["p_turned"], 1)
                    return step

                def mix(j):
                    def step(g, p, j2):
                        n, q = g * G + j, j % 2
                        pe.wait_ge(s["pt_kept"], n + 1)
                        if j == 0:
                            pe.wait_ge(s["v_ready"], g + 1)
                            pe.wait_ge(s["v_cls_ready"], g + 1)
                            wait(pe, s["y_ready"], g)
                        nc.tensor.matmul(p_y[0:S, j * D:(j + 1) * D], pt_cls[q][:], v_cls[p][:, j, :], start=True, stop=False)
                        for i in range(NH // 2):
                            c = j * D + i * 2 * DH
                            last = nc.tensor.matmul(p_y[0:S, c:c + 2 * DH], pt[q][:, i, :], v_pair[p][:, j, i, :], start=False, stop=i == NH // 2 - 1)
                        last.then_inc(s["mixed"], 1)
                    return step

                def turn_y(g, p, j2):
                    pe.wait_ge(s["yh_ready"], g + 1)
                    wait(pe, s["x_ready"], upto(g + 5, NG))
                    wait(pe, s["added"], g)
                    for j in range(G):
                        last = nc.tensor.transpose(pm0[:, j * S:(j + 1) * S], yh[:, j * NH:(j + 1) * NH, :].rearrange("p a b -> p (a b)"), ident[0:S, 0:S])
                    last.then_inc(s["y_turned"], 1)

                def out(g, p, j2):
                    pe.wait_ge(s["u_ready"], g + 1)
                    for j in range(G):
                        last = nc.tensor.matmul(pm0[0:S, j * D:(j + 1) * D], u[:, j * S:(j + 1) * S], wt["wo1"][:], start=True, stop=True)
                    last.then_inc(s["out_made"], 1)

                ticks(pe, NG, [
                    (2, score(0)), (1, make_q), (3, turn_p(1)), (3, mix(0)), (5, turn_y),
                    (2, score(1)), (1, make_k), (3, turn_p(2)), (3, mix(1)),
                    (2, score(2)), (1, make_v), (3, turn_p(3)), (3, mix(2)), (5, out),
                    (2, score(3)), (2, turn_p(0)), (3, mix(3)), (0, turn_x)])

def top2_gates(nc, io, st):
    ident, xt_all, comb = st["ident"], st["xt_all"], st["comb"]
    with ExitStack() as ctx:
        m = Mem(nc, ctx)
        wr, br = m.sb("m_wr", [D, E1]), m.sb("m_br", [S, E1])
        xn = [m.sb(f"m_xn{i}", [S, G, D]) for i in range(2)]
        xt = [m.sb(f"m_xt{i}", [D, W]) for i in range(2)]
        lg, ex, prob, rank = (m.sb(f"m_{n}", [S, B, E1]) for n in ("lg", "ex", "prob", "rank"))
        neg, inv = m.sb("m_neg", [S, B]), m.sb("m_inv", [S, B])
        beats = m.sb("m_beats", [S, B, E1, E1])
        p_x = [m.ps(f"m_px{i}", [D, W]) for i in range(2)]
        p_l = [m.ps(f"m_pl{i}", [S, G, E1]) for i in range(2)]
        ln = ln_statistics(nc, st, m, "m")
        w_in, zeroed, experts_in = m.sem("m_weights_in"), m.sem("m_beats_zeroed"), m.sem("m_experts_in")
        normed, x_turned, x_ready, x_kept = m.sem("m_normed"), m.sem("m_x_turned"), m.sem("m_x_ready"), m.sem("m_x_kept")
        gated, logits_kept, exped, chain = m.sem("m_gated"), m.sem("m_logits_kept"), m.sem("m_exped"), m.sem("m_chain")
        with nc.Block() as block:

            @block.sync
            def _(sp):
                sp.dma_start(wr[:], io["wr_t"]).then_inc(w_in, 16)
                sp.dma_start(br[:], row_broadcast(io["br"], S)).then_inc(w_in, 16)
                sp.dma_start(st["w1f"][:], io["W1"].rearrange("e d h -> d e h")).then_inc(experts_in, 16)
                sp.dma_start(st["w2f"][:], io["W2"].rearrange("e (c p) d -> p (e c) d", p=D)).then_inc(experts_in, 16)
                sp.wait_ge(experts_in, 32)

            @block.gpsimd
            def _(pool):
                nc.gpsimd.memset(beats[:], 0.0).then_inc(zeroed, 1)

            @block.vector
            def _(dve):
                ln_on_dve(nc, dve, ln)
                dve.wait_ge(w_in, 32)

                def norm(g, p, j2):
                    wait(dve, x_turned, g - 1)
                    normalise(nc, xn[p], st, g * G, G).then_inc(normed, 1)

                def keep_logits(g, p, j2):
                    dve.wait_ge(gated, g + 1)
                    nc.vector.tensor_tensor(lg[:, ds(g * G, G), :], p_l[p][:], bc(br[:], 1, G), ALU.add).then_inc(logits_kept, 1)

                ticks(dve, NG, [(2, keep_logits), (0, norm)])

                done = 0

                def then(ins):
                    nonlocal done
                    ins.then_inc(chain, 1)
                    done += 1
                    dve.wait_ge(chain, done)

                dve.wait_ge(logits_kept, NG)
                then(nc.vector.tensor_reduce(neg[:], lg[:], X, ALU.max, negate=True))
                then(nc.vector.tensor_tensor(lg[:], lg[:], bc(neg[:], 2, E1), ALU.add))
                dve.wait_ge(exped, 1)
                then(nc.vector.tensor_reduce(neg[:], ex[:], X, ALU.add))
                then(nc.vector.reciprocal(inv[:], neg[:]))
                then(nc.vector.tensor_tensor(prob[:], ex[:], bc(inv[:], 2, E1), ALU.mult))
                dve.wait_ge(zeroed, 1)
                for e in range(E1):
                    if e > 0:
                        last = nc.vector.tensor_tensor(beats[:, :, e, 0:e], prob[:, :, 0:e], bc(prob[:, :, e], 2, e), ALU.is_ge)
                    if e < E1 - 1:
                        last = nc.vector.tensor_tensor(beats[:, :, e, e + 1:E1], prob[:, :, e + 1:E1], bc(prob[:, :, e], 2, E1 - 1 - e), ALU.is_gt)
                then(last)
                then(nc.vector.tensor_reduce(rank[:], beats[:], X, ALU.add))
                then(nc.vector.scalar_tensor_tensor(out=ex[:], in0=rank[:], scalar=1.5, in1=prob[:], op0=ALU.is_lt, op1=ALU.mult))
                then(nc.vector.tensor_copy(comb[:, :, 0, :], ex[:]))
                then(nc.vector.tensor_tensor(prob[:], ex[:], comb[:, :, 0, :], ALU.subtract))
                then(nc.vector.tensor_copy(comb[:, :, 1, :], prob[:]))
                then(nc.vector.tensor_tensor(rank[:], prob[:], comb[:, :, 1, :], ALU.subtract))
                then(nc.vector.tensor_copy(comb[:, :, 2, :], rank[:]))

            @block.scalar
            def _(act):
                def keep_x(g, p, j2):
                    act.wait_ge(x_turned, g + 1)
                    wait(act, gated, g - 1)
                    nc.scalar.copy(xt[p][:], p_x[p][:]).then_inc(x_ready, 1)
                    nc.scalar.copy(xt_all[:, ds(g * G, G), :], p_x[p][:].rearrange("p (a b) -> p a b", a=G)).then_inc(x_kept, 1)

                ticks(act, NG, [(0, keep_x)])
                act.wait_ge(chain, 2)
                nc.scalar.activation(ex[:], lg[:], ACT.Exp).then_inc(exped, 1)

            @block.tensor
            def _(pe):
                pe.wait_ge(w_in, 32)

                def turn_x(g, p, j2):
                    pe.wait_ge(normed, g + 1)
                    wait(pe, x_kept, g - 1)
                    for j in range(G):
                        last = nc.tensor.transpose(p_x[p][:, j * S:(j + 1) * S], xn[p][:, j, :], ident[0:S, 0:S])
                    last.then_inc(x_turned, 1)

                def gates(g, p, j2):
                    pe.wait_ge(x_ready, g + 1)
                    wait(pe, logits_kept, g - 1)
                    for j in range(G):
                        last = nc.tensor.matmul(p_l[p][:, j, :], xt[p][:, j * S:(j + 1) * S], wr[:], start=True, stop=True)
                    last.then_inc(gated, 1)

                ticks(pe, NG, [(1, gates), (0, turn_x)])


def top2_layers(nc, io, st):
    h, ident, xt_all, comb = st["h"], st["ident"], st["xt_all"], st["comb"]
    NI = E1 * (H1 // D)
    ROWS = 3 * E1
    LOW, DOWN, HB = 2, 6, 8
    with ExitStack() as ctx:
        m = Mem(nc, ctx)
        w1f, w2f = st["w1f"], st["w2f"]
        w1 = [m.sb(f"n_w1_{i}", [D, E1, H1], F32R) for i in range(2)]
        w2 = [m.sb(f"n_w2_{i}", [D, NI, D], F32R) for i in range(2)]
        xs = [[m.sb(f"n_xs{i}{j}", [D, W], F32R) for j in range(2)] for i in range(2)]
        b1 = m.sb("n_b1", [D, NI])
        b2f, b2r = m.sb("n_b2f", [ROWS, D]), m.sb("n_b2r", [ROWS, D])
        b2 = [m.sb(f"n_b2_{i}", [ROWS, D], BF16) for i in range(3)]
        pickf, pick = m.sb("n_pickf", [ROWS, E1, D]), m.sb("n_pick", [ROWS, E1, D], BF16)
        identb = m.sb("n_identb", [S, S], BF16)
        cs = [m.sb(f"n_cs{i}", [S, G, ROWS], BF16) for i in range(2)]
        ct = [m.sb(f"n_ct{i}", [ROWS, W], BF16) for i in range(2)]
        hg = [m.sb(f"n_hg{i}", [D, W]) for i in range(4)]
        hs = [m.sb(f"n_hs{i}", [D, W]) for i in range(HB)]
        hsp = [[m.sb(f"n_hsp{i}{j}", [D, W], F32R) for j in range(2)] for i in range(HB)]
        yt = [m.sb(f"n_yt{i}", [D, W]) for i in range(2)]
        ho = [m.sb(f"n_ho{i}", [S, G, D]) for i in range(2)]
        p_h = [m.ps(f"n_ph{i}", [D, W]) for i in range(2)]
        p_b = [m.ps(f"n_pb{i}", [D, W]) for i in range(2)]
        p_y = [m.ps(f"n_py{i}", [D, W]) for i in range(2)]
        p_c, p_o = m.ps("n_pc", [ROWS, G, S + 1], BF16), m.ps("n_po", [S, G, D])
        sems = ("weights_in", "b2_split", "consts_ready", "cs_ready", "c_turned", "ct_ready", "hidden", "gate_spread", "gelu_done",
                "w_high", "w_low", "x_high", "x_low", "scaled", "high_by_act", "high_by_dve", "low_by_pool", "low_by_dve", "multiplied", "y_done", "yt_ready", "y_turned", "sum_ready")
        stored = [m.sem(f"n_stored{i}") for i in range(2)]
        s = {n: m.sem("n_" + n) for n in sems}
        n_in = 16 * 5

        def low_count(g, i, ahead=0):
            if i % 4 == 3:
                return s["low_by_dve"], g * (NI // 4) + (i + ahead) // 4 + 1
            return s["low_by_pool"], g * (NI * 3 // 4) + (i + ahead) // 4 * 3 + i % 4 + 1

        with nc.Block() as block:

            @block.sync
            def _(sp):
                sp.dma_start(b1[:], io["b1m_t"]).then_inc(s["weights_in"], 16)
                sp.dma_start(pickf[:], io["pick"]).then_inc(s["weights_in"], 16)
                for i in range(3):
                    sp.dma_start(b2f[i * E1:(i + 1) * E1, :], io["b2m"]).then_inc(s["weights_in"], 16)

                def put(g, p, j2):
                    sp.wait_ge(s["sum_ready"], g + 1)
                    sp.dma_start(io["out"][ds(g * G, G)].rearrange("b s d -> s b d"), ho[p][:]).then_inc(stored[p], 16)

                ticks(sp, NG, [(0, put)])
                for p in range(2):
                    sp.wait_ge(stored[p], NG // 2 * 16)

            @block.gpsimd
            def _(pool):
                pool.wait_ge(s["weights_in"], n_in)

                def stage(g, p, j2):
                    wait(pool, s["c_turned"], g - 1)
                    nc.gpsimd.tensor_copy(cs[p][:], comb[:, ds(g * G, G), :, :].rearrange("p a b c -> p a (b c)")).then_inc(s["cs_ready"], 1)

                def low(i):
                    by = s["high_by_dve"] if i % 2 else s["high_by_act"]

                    def step(g, p, j2):
                        pool.wait_ge(by, g * (NI // 2) + i // 2 + 1)
                        nc.gpsimd.tensor_tensor(hsp[i % HB][1][:], hs[i % HB][:], hsp[i % HB][0][:], ALU.subtract).then_inc(s["low_by_pool"], 1)
                    return step

                ticks(pool, NG, [(0, stage)] + [(2 if i < LOW else 1, low((i - LOW) % NI)) for i in range(NI) if (i - LOW) % 4 != 3])

            @block.vector
            def _(dve):
                dve.wait_ge(s["weights_in"], n_in)
                dve.wait_ge(s["w_high"], 2)
                nc.vector.tensor_tensor(w1[1][:], w1f[:], w1[0][:], ALU.subtract)
                nc.vector.tensor_tensor(w2[1][:], w2f[:], w2[0][:], ALU.subtract).then_inc(s["w_low"], 1)
                nc.vector.tensor_copy(identb[:], ident[0:S, 0:S])
                nc.vector.tensor_copy(pick[:], pickf[:])
                nc.vector.tensor_copy(b2[0][:], b2f[:]).then_inc(s["b2_split"], 1)
                dve.wait_ge(s["b2_split"], 1)
                nc.vector.tensor_tensor(b2r[:], b2f[:], b2[0][:], ALU.subtract).then_inc(s["b2_split"], 1)
                dve.wait_ge(s["b2_split"], 2)
                nc.vector.tensor_copy(b2[1][:], b2r[:]).then_inc(s["b2_split"], 1)
                dve.wait_ge(s["b2_split"], 3)
                nc.vector.tensor_tensor(b2f[:], b2r[:], b2[1][:], ALU.subtract).then_inc(s["b2_split"], 1)
                dve.wait_ge(s["b2_split"], 4)
                nc.vector.tensor_copy(b2[2][:], b2f[:]).then_inc(s["consts_ready"], 1)

                def high_x(g, p, j2):
                    wait(dve, s["multiplied"], (g - 1) * NI - DOWN)
                    nc.vector.tensor_copy(xs[p][0][:].rearrange("p (a b) -> p a b", a=G), xt_all[:, ds(g * G, G), :]).then_inc(s["x_high"], 1)

                def low_x(g, p, j2):
                    dve.wait_ge(s["x_high"], g + 1)
                    nc.vector.tensor_tensor(xs[p][1][:].rearrange("p (a b) -> p a b", a=G), xt_all[:, ds(g * G, G), :],
                                            xs[p][0][:].rearrange("p (a b) -> p a b", a=G), ALU.subtract).then_inc(s["x_low"], 1)

                def scale(i):
                    def step(g, p, j2):
                        n = g * NI + i
                        dve.wait_ge(s["gelu_done"], n + 1)
                        if i % 2 == 0:
                            dve.wait_ge(s["gate_spread"], g * E1 + i // 2 + 1)
                        wait(dve, *low_count(g, i, -HB))
                        nc.vector.tensor_tensor(hs[i % HB][:], hg[i % 4][:], p_b[i // 2 % 2][:], ALU.mult).then_inc(s["scaled"], 1)
                    return step

                def high(i):
                    def step(g, p, j2):
                        n = g * NI + i
                        dve.wait_ge(s["scaled"], n + 1)
                        wait(dve, s["multiplied"], n - HB + 1)
                        nc.vector.tensor_copy(hsp[i % HB][0][:], hs[i % HB][:]).then_inc(s["high_by_dve"], 1)
                    return step

                def low(i):
                    def step(g, p, j2):
                        dve.wait_ge(s["high_by_dve"], g * (NI // 2) + i // 2 + 1)
                        nc.vector.tensor_tensor(hsp[i % HB][1][:], hs[i % HB][:], hsp[i % HB][0][:], ALU.subtract).then_inc(s["low_by_dve"], 1)
                    return step

                def add(g, p, j2):
                    dve.wait_ge(s["y_turned"], g + 1)
                    wait(dve, stored[p], j2 * 16)
                    nc.vector.tensor_tensor(ho[p][:], h[:, ds(g * G, G), :], p_o[:], ALU.add).then_inc(s["sum_ready"], 1)

                steps = []
                for i in range(NI):
                    steps.append((1, scale(i)))
                    if i % 4 == 1:
                        steps.append((2 if i == 1 else 1, low((i - 2) % NI)))
                    if i % 2 == 0:
                        steps.append((2 if i == 0 else 1, high((i - 1) % NI)))
                    if i == 14:
                        steps.append((2, add))
                    if i == 6:
                        steps.append((0, high_x))
                    if i == 10:
                        steps.append((0, low_x))
                ticks(dve, NG, steps)

            @block.scalar
            def _(act):
                act.wait_ge(s["weights_in"], n_in)
                for high, full in ((w1[0], w1f), (w2[0], w2f)):
                    nc.scalar.copy(high[:], full[:]).then_inc(s["w_high"], 1)

                def gelu(i):
                    def step(g, p, j2):
                        n = g * NI + i
                        act.wait_ge(s["hidden"], n + 1)
                        wait(act, s["scaled"], n - 3)
                        nc.scalar.activation(hg[i % 4][:], p_h[i % 2][:], ACT.Gelu, bias=b1[:, i:i + 1]).then_inc(s["gelu_done"], 1)
                    return step

                def keep_gates(g, p, j2):
                    act.wait_ge(s["c_turned"], g + 1)
                    wait(act, s["y_done"], g - 1)
                    nc.scalar.copy(ct[p][:].rearrange("p (a b) -> p a b", a=G), p_c[:, :, 0:S]).then_inc(s["ct_ready"], 1)

                def keep_y(g, p, j2):
                    act.wait_ge(s["y_done"], g + 1)
                    wait(act, s["y_turned"], g - 1)
                    nc.scalar.copy(yt[p][:], p_y[p][:]).then_inc(s["yt_ready"], 1)

                def high(i):
                    def step(g, p, j2):
                        n = g * NI + i
                        act.wait_ge(s["scaled"], n + 1)
                        wait(act, s["multiplied"], n - HB + 1)
                        nc.scalar.copy(hsp[i % HB][0][:], hs[i % HB][:]).then_inc(s["high_by_act"], 1)
                    return step

                steps = []
                for i in range(NI):
                    steps.append((1, gelu(i)))
                    if i % 2 == 1:
                        steps.append((1, high(i - 1)))
                    if i == 7:
                        steps.append((2, keep_y))
                    if i == 11:
                        steps.append((0, keep_gates))
                ticks(act, NG, steps)

            @block.tensor
            def _(pe):
                pe.wait_ge(s["weights_in"], n_in)
                pe.wait_ge(s["consts_ready"], 1)
                pe.wait_ge(s["w_low"], 1)

                def product(out, w, x, first, last):
                    for i, j in ((0, 0), (0, 1), (1, 0)):
                        ins = nc.tensor.matmul(out, w[i], x[j], start=first and i + j == 0, stop=last and i == 1)
                    return ins

                def turn_gates(g, p, j2):
                    pe.wait_ge(s["cs_ready"], g + 1)
                    wait(pe, s["ct_ready"], g)
                    for j in range(G):
                        last = nc.tensor.transpose(p_c[:, j, 0:S], cs[p][:, j, :], identb[:])
                    last.then_inc(s["c_turned"], 1)

                def up(i):
                    def step(g, p, j2):
                        n, e = g * NI + i, i // 2
                        if i == 0:
                            pe.wait_ge(s["ct_ready"], g + 1)
                            pe.wait_ge(s["x_low"], g + 1)
                        if i % 2 == 0:
                            wait(pe, s["scaled"], n - 2)
                            nc.tensor.matmul(p_b[e % 2][:], pick[:, e, :], ct[p][:], start=True, stop=True).then_inc(s["gate_spread"], 1)
                        wait(pe, s["gelu_done"], n - 1)
                        product(p_h[i % 2][:], [t[:, e, i % 2 * D:(i % 2 + 1) * D] for t in w1], [t[:] for t in xs[p]], True, True).then_inc(s["hidden"], 1)
                    return step

                def down(i):
                    def step(g, p, j2):
                        n = g * NI + i
                        pe.wait_ge(*low_count(g, i))
                        if i == 0:
                            wait(pe, s["yt_ready"], g - 1)
                        product(p_y[p][:], [t[:, i, :] for t in w2], [t[:] for t in hsp[i % HB]], i == 0, False).then_inc(s["multiplied"], 1)
                        if i == NI - 1:
                            for k in range(3):
                                last = nc.tensor.matmul(p_y[p][:], b2[k][:], ct[p][:], start=False, stop=k == 2)
                            last.then_inc(s["y_done"], 1)
                    return step

                def turn_y(g, p, j2):
                    pe.wait_ge(s["yt_ready"], g + 1)
                    wait(pe, s["sum_ready"], g)
                    for j in range(G):
                        last = nc.tensor.transpose(p_o[:, j, :], yt[p][:, j * S:(j + 1) * S], ident[:])
                    last.then_inc(s["y_turned"], 1)

                steps = []
                for i in range(NI):
                    steps += [(1, up(i)), (2 if i < DOWN else 1, down((i - DOWN) % NI))]
                    if i == 6:
                        steps.append((0, turn_gates))
                    if i == 10:
                        steps.append((2, turn_y))
                ticks(pe, NG, steps)


def top2_experts(nc, io, st):
    with ExitStack() as ctx:
        m = Mem(nc, ctx)
        st = dict(st, xt_all=m.sb("xt_all", [D, B, S]), comb=m.sb("comb", [S, B, 3, E1], BF16),
                  w1f=m.sb("n_w1f", [D, E1, H1]), w2f=m.sb("n_w2f", [D, E1 * H1 // D, D]))
        top2_gates(nc, io, st)
        top2_layers(nc, io, st)


def tower(nc, io):
    with ExitStack() as ctx:
        m = Mem(nc, ctx)
        st = {
            "h": m.sb("h", [S, B, D]),
            "stats": m.sb("stats", [S, B, 6]),
            "ident": m.sb("ident", [128, 128]),
            "mean": m.sb("mean", [S, B]),
            "rstd": m.sb("rstd", [S, B]),
            "minus_half": m.sb("minus_half", [S, B]),
        }
        patch_tokens(nc, io, st)
        attention(nc, io, st)
        expert_choice(nc, io, st)
        retention(nc, io, st)
        top2_experts(nc, io, st)


def constants():
    f = np.float32
    pos = np.arange(S, dtype=f)[:, None]
    div = np.exp(np.arange(0, D, 2, dtype=f) * f(-np.log(10000.0) / D)).astype(f)
    ang = pos * div
    sinus_t = np.concatenate([np.sin(ang), np.cos(ang)], axis=-1).astype(f).T
    sv = (np.arange(0, DH, 2, dtype=f) + f(0.4 * DH)) / f(1.4 * DH)
    scale = (sv[None, :] ** (np.arange(S, dtype=f) / f(128))[:, None]).astype(f)
    ang1 = np.arange(S, dtype=f)[:, None] * (f(1) / f(10000) ** (np.arange(DH // 2, dtype=f) / f(DH // 2)))[None, :]
    sign = np.tile(np.array([-1, 1], f), D // 2)[:, None]
    tab = {}
    for n, sc in (("q", scale), ("k", f(1) / scale)):
        tab[f"cos_{n}"] = np.tile(np.repeat(np.cos(ang1) * sc, 2, axis=1), (1, NH)).T.astype(f)
        tab[f"sin_{n}"] = np.tile(np.repeat(np.sin(ang1) * sc, 2, axis=1), (1, NH)).T.astype(f) * sign
    gammas = (1 - np.exp(np.linspace(np.log(1 / 32), np.log(1 / 128), NH))).astype(f)
    dist = np.abs(np.arange(S)[:, None] - np.arange(S)[None, :]).astype(f)
    tab["decay"] = (gammas[None, :, None] ** dist[:, None, :]).astype(f).reshape(S, 2, NH // 2, S)
    tab["head_mask"] = np.stack([(np.arange(D) // DH % 2 == i) for i in range(2)], axis=1).astype(f)
    tab["own_channels"] = np.repeat(np.eye(NH, dtype=f), DH, axis=1)
    tab["pick"] = np.repeat(np.tile(np.eye(E1, dtype=f), (3, 1))[:, :, None], D, axis=2)
    return {**tab, "sinus_t": np.ascontiguousarray(sinus_t), "iota": np.arange(S, dtype=f)}


def heads(w):
    return w.transpose(1, 0, 2).reshape(D, D)


def kernel(**inputs):
    import concourse.bacc as bacc
    from concourse.bass_utils import run_bass_kernel_spmd

    a = {k: np.asarray(v) for k, v in inputs.items()}
    img = a["x"].reshape(B // TI, TI, 3, PY, PATCH, PY, PATCH)
    data = {
        "patches": img.transpose(0, 2, 4, 6, 1, 3, 5).reshape(B // TI, IN_D, TN),
        "tok_wt": a["L0_tok_W"].T,
        "pos_t": a["L0_tok_pos_embed"].T,
        "tok_b": a["L0_tok_b"],
        "cls_t": a["L0_tok_class_token"].T,
        "wq_t": a["L0_attn_Wq"].T, "wk_t": a["L0_attn_Wk"].T, "wv_t": a["L0_attn_Wv"].T,
        "gate": a["L0_ffn_gate_weight"], "w1": a["L0_ffn_w1"], "w2": a["L0_ffn_w2"], "b1_t": a["L0_ffn_b1"].T, "b2_t": a["L0_ffn_b2"].T,
        "bq": a["L0_attn_bq"], "bk": a["L0_attn_bk"], "bv": a["L0_attn_bv"],
        "wv1": heads(a["L1_attn_W_V"]), "wg1": a["L1_attn_W_G"], "wo1": a["L1_attn_W_O"],
        "gnw": a["L1_attn_gn_weight"], "gnb": a["L1_attn_gn_bias"],
    }
    data.update({
        "wr_t": a["L1_ffn_Wr"].T, "br": a["L1_ffn_br"], "W1": a["L1_ffn_W1"], "W2": a["L1_ffn_W2"],
        "b1m_t": a["L1_ffn_b1"].reshape(E1 * H1 // D, D).T, "b2m": a["L1_ffn_b2"],
    })
    for n in "qk":
        data[f"w{n}1"] = heads(a[f"L1_attn_W_{n.upper()}"])
        data[f"w{n}1_turn"] = data[f"w{n}1"].reshape(D, D // 2, 2)[:, :, ::-1].reshape(D, D)
    data.update(constants())
    nc = bacc.Bacc("TRN2", target_bir_lowering=False, num_devices=1)
    arrays, io = {}, {}
    for name, v in data.items():
        arrays[f"in_{name}"] = np.ascontiguousarray(v)
        io[name] = nc.dram_tensor(f"in_{name}", v.shape, mybir.dt.from_np(v.dtype), kind="ExternalInput").ap()
    io["out"] = nc.dram_tensor("out_0", (B, S, D), F32, kind="ExternalOutput").ap()
    tower(nc, io)
    return run_bass_kernel_spmd(nc, [arrays], core_ids=[0]).results[0]["out_0"]
```
